# Optimizing a Trainium2 kernel written in Bass

```python
import numpy as np
import jax
import jax.numpy as jnp

def _softmax(x, axis=-1):
    return jax.nn.softmax(x, axis=axis)

def _gelu(x):
    return jax.nn.gelu(x, approximate=True)

def _silu(x):
    return jax.nn.silu(x)

def _sigmoid(x):
    return jax.nn.sigmoid(x)

def _layernorm(x, axis=-1, eps=1e-05):
    m = jnp.mean(x, axis=axis, keepdims=True)
    v = jnp.var(x, axis=axis, keepdims=True)
    return (x - m) / jnp.sqrt(v + eps)

def _scatter_add(tgt, idx, src, axis=0):
    return tgt.at[idx].add(src)

def _segment_sum(src, seg, n):
    return jax.ops.segment_sum(src, seg, n)
kernel_name = 'mk_vit_tower_d1_tok_img768_r4_baa32f'

def setup_inputs(seed: int=0):
    np.random.seed(seed)
    _w = jnp.asarray

    def _rec_inputs():
        import jax
        import jax.numpy as jnp
        _rk = jax.random.key(seed)
        x = -0.000356955 + 1 * jax.random.normal(jax.random.fold_in(_rk, 1), (128, 3, 64, 64), jnp.float32)
        return x
    x = _rec_inputs()

    def _L0_tok_setup():
        import jax, jax.numpy as jnp
        import numpy as np
        PATCH = 16
        EMBED = 192
        IN_DIM = PATCH * PATCH * 3

        def extract_patches(x, p):
            B, C, H, Wd = x.shape
            h, w = (H // p, Wd // p)
            xr = x.reshape(B, C, h, p, w, p)
            xr = xr.transpose(0, 2, 4, 3, 5, 1)
            return xr.reshape(B, h * w, p * p * C)
        key = jax.random.key(seed)
        kx, kw, kb = jax.random.split(key, 3)
        x = jax.random.normal(kx, (128, 3, 224, 224), dtype=jnp.float32)
        bound = 1.0 / np.sqrt(IN_DIM)
        W = jax.random.uniform(kw, (EMBED, IN_DIM), jnp.float32, -bound, bound)
        b = jax.random.uniform(kb, (EMBED,), jnp.float32, -bound, bound)
        return {'x': x, 'W': W, 'b': b}
    _L0_tok_all = _L0_tok_setup()
    _L0_tok_in = {k: v for k, v in _L0_tok_all.items() if k in ('W', 'b')}
    del _L0_tok_all

    def _L0_attn_setup():
        import jax, jax.numpy as jnp
        import numpy as np
        N_HEAD = 12

        def _rotate_half(x):
            x_even = x[..., ::2]
            x_odd = x[..., 1::2]
            return jnp.stack((-x_odd, x_even), axis=-1).reshape(x.shape)

        def _rope_tables(T, D, dtype):
            inv_freq = 1.0 / 10000.0 ** (jnp.arange(0, D, 2, dtype=jnp.float32) / D)
            freqs = jnp.arange(T, dtype=jnp.float32)[:, None] * inv_freq[None, :]
            cos = jnp.repeat(jnp.cos(freqs), 2, axis=-1).astype(dtype)
            sin = jnp.repeat(jnp.sin(freqs), 2, axis=-1).astype(dtype)
            return (cos, sin)
        key = jax.random.key(seed)
        ks = jax.random.split(key, 5)
        B, T, C = (8, 256, 192)
        return {'x': jax.random.normal(ks[0], (B, T, C), dtype=jnp.float32), 'W_attn': jax.random.normal(ks[1], (C, 3 * C), dtype=jnp.float32) * C ** (-0.5), 'b_attn': jax.random.normal(ks[2], (3 * C,), dtype=jnp.float32) * 0.02, 'W_proj': jax.random.normal(ks[3], (C, C), dtype=jnp.float32) * C ** (-0.5), 'b_proj': jax.random.normal(ks[4], (C,), dtype=jnp.float32) * 0.02}
    _L0_attn_all = _L0_attn_setup()
    _L0_attn_in = {k: v for k, v in _L0_attn_all.items() if k in ('W_attn', 'b_attn', 'W_proj', 'b_proj')}
    del _L0_attn_all

    def _L0_ffn_setup():
        import jax, jax.numpy as jnp
        import numpy as np
        E = 16
        K = 4
        H = 192
        I = 384
        LIMIT = 7.0
        ALPHA = 1.702
        EPS = 1e-05

        def rmsnorm(x, scale):
            xf = x.astype(jnp.float32)
            inv = jax.lax.rsqrt(jnp.mean(xf * xf, axis=-1, keepdims=True) + EPS)
            return (xf * inv).astype(x.dtype) * scale

        def swiglu(x, limit=LIMIT, alpha=ALPHA):
            x_glu = x[..., ::2]
            x_lin = x[..., 1::2]
            x_glu = jnp.minimum(x_glu, limit)
            x_lin = jnp.clip(x_lin, -limit, limit)
            return x_glu * jax.nn.sigmoid(alpha * x_glu) * (x_lin + 1.0)
        key = jax.random.key(seed)
        ks = jax.random.split(key, 7)
        s = 0.02
        return {'x': jax.random.normal(ks[0], (2, 256, H), dtype=jnp.float32), 'norm_scale': jnp.ones((H,), dtype=jnp.float32), 'gate_w': jax.random.normal(ks[1], (E, H), dtype=jnp.float32) * s, 'gate_b': jnp.zeros((E,), dtype=jnp.float32), 'mlp1_w': jax.random.normal(ks[2], (E, 2 * I, H), dtype=jnp.float32) * s, 'mlp1_b': jax.random.normal(ks[3], (E, 2 * I), dtype=jnp.float32) * s, 'mlp2_w': jax.random.normal(ks[4], (E, H, I), dtype=jnp.float32) * s, 'mlp2_b': jax.random.normal(ks[5], (E, H), dtype=jnp.float32) * s}
    _L0_ffn_all = _L0_ffn_setup()
    _L0_ffn_in = {k: v for k, v in _L0_ffn_all.items() if k in ('norm_scale', 'gate_w', 'gate_b', 'mlp1_w', 'mlp1_b', 'mlp2_w', 'mlp2_b')}
    del _L0_ffn_all
    return {'x': x, 'L0_tok_W': _L0_tok_in['W'], 'L0_tok_b': _L0_tok_in['b'], 'L0_attn_W_attn': _L0_attn_in['W_attn'], 'L0_attn_b_attn': _L0_attn_in['b_attn'], 'L0_attn_W_proj': _L0_attn_in['W_proj'], 'L0_attn_b_proj': _L0_attn_in['b_proj'], 'L0_ffn_norm_scale': _L0_ffn_in['norm_scale'], 'L0_ffn_gate_w': _L0_ffn_in['gate_w'], 'L0_ffn_gate_b': _L0_ffn_in['gate_b'], 'L0_ffn_mlp1_w': _L0_ffn_in['mlp1_w'], 'L0_ffn_mlp1_b': _L0_ffn_in['mlp1_b'], 'L0_ffn_mlp2_w': _L0_ffn_in['mlp2_w'], 'L0_ffn_mlp2_b': _L0_ffn_in['mlp2_b']}

def reference(x, L0_tok_W, L0_tok_b, L0_attn_W_attn, L0_attn_b_attn, L0_attn_W_proj, L0_attn_b_proj, L0_ffn_norm_scale, L0_ffn_gate_w, L0_ffn_gate_b, L0_ffn_mlp1_w, L0_ffn_mlp1_b, L0_ffn_mlp2_w, L0_ffn_mlp2_b):
    import jax
    import jax.numpy as jnp

    def _L0_tok_ref(x, W, b):
        import jax, jax.numpy as jnp
        import numpy as np
        PATCH = 16
        EMBED = 192
        IN_DIM = PATCH * PATCH * 3

        def extract_patches(x, p):
            B, C, H, Wd = x.shape
            h, w = (H // p, Wd // p)
            xr = x.reshape(B, C, h, p, w, p)
            xr = xr.transpose(0, 2, 4, 3, 5, 1)
            return xr.reshape(B, h * w, p * p * C)
        patches = extract_patches(x, PATCH)
        return jnp.einsum('bnd,ed->bne', patches, W) + b

    def _L0_attn_ref(x, W_attn, b_attn, W_proj, b_proj):
        import jax, jax.numpy as jnp
        import numpy as np
        N_HEAD = 12

        def _rotate_half(x):
            x_even = x[..., ::2]
            x_odd = x[..., 1::2]
            return jnp.stack((-x_odd, x_even), axis=-1).reshape(x.shape)

        def _rope_tables(T, D, dtype):
            inv_freq = 1.0 / 10000.0 ** (jnp.arange(0, D, 2, dtype=jnp.float32) / D)
            freqs = jnp.arange(T, dtype=jnp.float32)[:, None] * inv_freq[None, :]
            cos = jnp.repeat(jnp.cos(freqs), 2, axis=-1).astype(dtype)
            sin = jnp.repeat(jnp.sin(freqs), 2, axis=-1).astype(dtype)
            return (cos, sin)
        B, T, C = x.shape
        H = N_HEAD
        D = C // H
        qkv = x @ W_attn + b_attn
        q, k, v = jnp.split(qkv, 3, axis=-1)
        q = q.reshape(B, T, H, D).transpose(0, 2, 1, 3)
        k = k.reshape(B, T, H, D).transpose(0, 2, 1, 3)
        v = v.reshape(B, T, H, D).transpose(0, 2, 1, 3)
        cos, sin = _rope_tables(T, D, x.dtype)
        q = q * cos + _rotate_half(q) * sin
        k = k * cos + _rotate_half(k) * sin
        att = jnp.einsum('bhqd,bhkd->bhqk', q, k) * D ** (-0.5)
        causal = jnp.tril(jnp.ones((T, T), dtype=bool))
        att = jnp.where(causal, att, -jnp.inf)
        att = jax.nn.softmax(att, axis=-1)
        y = jnp.einsum('bhqk,bhkd->bhqd', att, v)
        y = y.transpose(0, 2, 1, 3).reshape(B, T, C)
        return y @ W_proj + b_proj

    def _L0_ffn_ref(x, norm_scale, gate_w, gate_b, mlp1_w, mlp1_b, mlp2_w, mlp2_b):
        import jax, jax.numpy as jnp
        import numpy as np
        E = 16
        K = 4
        H = 192
        I = 384
        LIMIT = 7.0
        ALPHA = 1.702
        EPS = 1e-05

        def rmsnorm(x, scale):
            xf = x.astype(jnp.float32)
            inv = jax.lax.rsqrt(jnp.mean(xf * xf, axis=-1, keepdims=True) + EPS)
            return (xf * inv).astype(x.dtype) * scale

        def swiglu(x, limit=LIMIT, alpha=ALPHA):
            x_glu = x[..., ::2]
            x_lin = x[..., 1::2]
            x_glu = jnp.minimum(x_glu, limit)
            x_lin = jnp.clip(x_lin, -limit, limit)
            return x_glu * jax.nn.sigmoid(alpha * x_glu) * (x_lin + 1.0)
        B, T, _ = x.shape
        t = rmsnorm(x, norm_scale)
        g = jnp.einsum('bth,eh->bte', t, gate_w) + gate_b
        top_vals, top_idx = jax.lax.top_k(g, K)
        route_w = jax.nn.softmax(top_vals, axis=-1)
        t_flat = t.reshape(B * T, H)
        idx_flat = top_idx.reshape(B * T, K)
        w_flat = route_w.reshape(B * T, K)
        onehot = jax.nn.one_hot(idx_flat, E, dtype=t_flat.dtype)
        comb = jnp.einsum('nke,nk->ne', onehot, w_flat)
        h = jnp.einsum('nh,ech->nec', t_flat, mlp1_w) + mlp1_b
        a = swiglu(h)
        y = jnp.einsum('nec,ehc->neh', a, mlp2_w) + mlp2_b
        out_flat = jnp.einsum('neh,ne->nh', y, comb)
        return x + out_flat.reshape(B, T, H)
    h = _L0_tok_ref(x, L0_tok_W, L0_tok_b)
    h = h + _L0_attn_ref(_layernorm(h, axis=-1), L0_attn_W_attn, L0_attn_b_attn, L0_attn_W_proj, L0_attn_b_proj)
    h = h + _L0_ffn_ref(_layernorm(h, axis=-1), L0_ffn_norm_scale, L0_ffn_gate_w, L0_ffn_gate_b, L0_ffn_mlp1_w, L0_ffn_mlp1_b, L0_ffn_mlp2_w, L0_ffn_mlp2_b)
    return h

_drawn_inputs = setup_inputs


def setup_inputs(seed=0):
    import zlib

    import numpy as np

    out = dict(_drawn_inputs(seed))
    spreads = {'L0_ffn_norm_scale': (1.0, 0.6), 'L0_ffn_gate_b': (0.0, 0.755)}
    factors = {'L0_ffn_gate_w': 3.59,
     'L0_ffn_mlp1_w': 3.26,
     'L0_ffn_mlp1_b': 8.0,
     'L0_ffn_mlp2_w': 3.166,
     'L0_ffn_mlp2_b': 8.0}
    for name, (base, spread) in spreads.items():
        noise = np.random.default_rng([zlib.crc32(name.encode()), seed]).standard_normal(out[name].shape)
        drawn = base * np.exp(spread * noise) if base else spread * noise
        out[name] = jnp.asarray(drawn.astype(out[name].dtype))
    for name, factor in factors.items():
        out[name] = (out[name] * factor).astype(out[name].dtype)
    return out
```

```python
from contextlib import ExitStack

import numpy as np

import concourse.bass as bass
from concourse import mybir

ALU = mybir.AluOpType
ACT = mybir.ActivationFunctionType
AX_X = mybir.AxisListType.X
F32 = mybir.dt.float32
BF16 = mybir.dt.bfloat16
I32 = mybir.dt.int32
U32 = mybir.dt.uint32

P = 128
TOKENS = 2048
TILES = TOKENS // P
SEQ = 16
IMGS = P // SEQ
DIM = 192
HALF = DIM // 2
PATCH = 768
PCH = PATCH // P
HEADS, HD = 12, 16
HH = HEADS // 2
EXPERTS, TOPK = 16, 4
INNER = 384
ICH = INNER // P
EPS = 1e-5
LIMIT, ALPHA = 7.0, 1.702
NEG = -1e30

REGION = TOKENS + P
SPARE = EXPERTS * REGION
SLOTS = TOKENS * TOPK // P + EXPERTS - 1
ROW = 212
W_AT, ID_AT = DIM, DIM + EXPERTS

PAD_SPLIT = (0, 6, 12, 16)
TABLE_STEPS = 12
GROUP = 32
YCH = HEADS // (P // GROUP)
V_N = DIM + HD
STAGES = 7
R_STAGES = 3

C_COLS = {}
_at = 0
for _name, _n in (("ident", P), ("cos", HD), ("sin", HD), ("head", HH), ("image", IMGS), ("causal", SEQ),
                  ("expert", EXPERTS), ("region", EXPERTS), ("grow", EXPERTS), ("tile", 1), ("pad", 1),
                  ("before", P), ("token", TILES)):
    C_COLS[_name] = (_at, _at + _n)
    _at += _n
C_N = _at


def shape_constants():
    c = np.zeros((P, C_N), np.float32)

    def put(name, value):
        a, b = C_COLS[name]
        c[:, a:b] = value

    p = np.arange(P)
    inv = (1.0 / np.float32(10000.0) ** (np.arange(0, HD, 2, dtype=np.float32) / np.float32(HD))).astype(np.float32)
    angle = ((p % SEQ).astype(np.float32)[:, None] * inv[None, :]).astype(np.float32)
    put("ident", np.eye(P))
    put("cos", np.repeat(np.cos(angle), 2, axis=1))
    put("sin", np.repeat(np.sin(angle), 2, axis=1) * np.tile([-1.0, 1.0], HD // 2))
    put("head", (p[:, None] // HD) == np.arange(HH)[None, :])
    put("image", (p[:, None] // SEQ) == np.arange(IMGS)[None, :])
    put("causal", np.where(np.arange(SEQ)[None, :] > (p % SEQ)[:, None], NEG, 0.0))
    put("expert", np.arange(EXPERTS)[None, :])
    put("region", np.arange(EXPERTS)[None, :] * REGION)
    put("grow", REGION)
    put("tile", p[:, None])
    put("pad", TOKENS + p[:, None])
    put("before", p[:, None] < p[None, :])
    put("token", p[:, None] + P * np.arange(TILES)[None, :])
    return c


def build(nc, x, consts, w_tok, b_tok, w_qkv, b_qkv, w_proj, nscale, w_gate, b_gate,
          w1, b1, w2, b2, out):
    routed = nc.dram_tensor("routed_rows", (SPARE + P, ROW), F32, kind="Internal").ap()
    with ExitStack() as ctx:
        def sb(name, shape, dt=F32):
            return ctx.enter_context(nc.sbuf_tensor(name, shape, dt))

        def bank(name):
            return ctx.enter_context(nc.psum_tensor(name, [P, 512], F32))

        def sem(name):
            return ctx.enter_context(nc.semaphore(name))

        banks = [bank(f"bank{i}") for i in range(8)]

        cst = sb("cst", [P, C_N])

        def const(name, rows=P):
            a, b = C_COLS[name]
            return cst[0:rows, a:b]

        ident = const("ident")
        w1_sb = sb("w1_sb", [HALF + 1, 2, EXPERTS, 2 * INNER])
        w2_sb = sb("w2_sb", [P, EXPERTS, ICH, DIM])
        wtok_sb = sb("wtok_sb", [P, PCH, DIM])
        wqkv_sb = sb("wqkv_sb", [HALF + 1, 2, 3 * DIM])
        wproj_sb = sb("wproj_sb", [P, YCH, DIM])
        wgate_sb = sb("wgate_sb", [HALF + 1, 2, EXPERTS])
        b2_sb = sb("b2_sb", [EXPERTS, DIM])
        btok_bc = sb("btok_bc", [P, DIM])
        nscale_bc = sb("nscale_bc", [P, DIM])
        power = sb("power", [P, 1])
        ones_bf = sb("ones_bf", [P, P], BF16)
        before_bf = sb("before_bf", [P, P], BF16)
        token_i = sb("token_i", [P, TILES], I32)
        pad_row = sb("pad_row", [P, ROW])
        h0 = sb("h0", [P, TILES, DIM])
        base = h0
        v_sb = sb("v_sb", [P, 2, 2 * DIM])

        x_sb = [sb(f"x_sb{i}", [P, PCH, P]) for i in range(2)]
        stats1, mv1, ve1, rstd1 = sb("stats1", [P, 6]), sb("mv1", [P, 2]), sb("ve1", [P, 1]), sb("rstd1", [P, 1])
        xn = sb("xn", [P, DIM])
        xnT = sb("xnT", [HALF + 1, 2, P])
        rope_c, rope_s = sb("rope_c", [P, 2 * DIM]), sb("rope_s", [P, 2 * DIM])
        qk = sb("qk", [P, 2 * DIM])
        kT = sb("kT", [HALF, 2, P])
        q_spread_all = sb("q_spread", [P, 2, IMGS, HH * SEQ])
        q_spread = q_spread_all[0:HALF]
        sc1, sc2, prob, probn = (sb(n, [HALF, 2 * IMGS, SEQ]) for n in ("sc1", "sc2", "prob", "probn"))
        rmax, rsum, rinv = (sb(n, [HALF, 2 * IMGS]) for n in ("rmax", "rsum", "rinv"))
        p_spread = sb("p_spread", [P, HEADS, P])
        yT = sb("yT", [P, YCH, P])
        h1 = sb("h1", [P, DIM])
        stats2, mv2, ve2, rstd2 = sb("stats2", [P, 6]), sb("mv2", [P, 2]), sb("ve2", [P, 1]), sb("rstd2", [P, 1])
        x2, x2sq = sb("x2", [P, DIM]), sb("x2sq", [P, DIM])
        ssq, msq, rms = sb("ssq", [P, 1]), sb("msq", [P, 1]), sb("rms", [P, 1])
        t_row = [sb(f"t_row{i}", [P, DIM]) for i in range(2)]
        packet = [sb(f"packet{i}", [P, ROW]) for i in range(2)]
        tT = sb("tT", [HALF + 1, 2, P])
        top_v, top_i, top_f = sb("top_v", [P, 8]), sb("top_i", [P, 8], U32), sb("top_f", [P, TOPK])
        top_d, top_e, top_w = sb("top_d", [P, TOPK]), sb("top_e", [P, TOPK]), sb("top_w", [P, TOPK])
        esum, einv = sb("esum", [P, 1]), sb("einv", [P, 1])
        onehot = sb("onehot", [P, TOPK, EXPERTS])
        onehot_w = sb("onehot_w", [P, TOPK, EXPERTS])
        onehot_r = sb("onehot_r", [P, TOPK, EXPERTS])
        comb = sb("comb", [P, EXPERTS])
        combT = sb("combT", [EXPERTS, P])
        chosen = sb("chosen", [P, EXPERTS], BF16)
        chosen_before = sb("chosen_before", [P, EXPERTS], BF16)
        place = sb("place", [P, EXPERTS])
        row_f = sb("row_f", [P, TOPK])
        row_i = [sb(f"row_i{i}", [P, TOPK], I32) for i in range(2)]

        cnt = sb("cnt", [P, EXPERTS])
        cnt_i, cnt_i2 = sb("cnt_i", [P, EXPERTS], I32), sb("cnt_i2", [P, EXPERTS], I32)
        fill_i = sb("fill_i", [1, EXPERTS], I32)
        ntile, tend = sb("ntile", [P, EXPERTS]), sb("tend", [P, EXPERTS])
        passed, jump, jumped = sb("passed", [P, EXPERTS]), sb("jump", [P, EXPERTS]), sb("jumped", [P, EXPERTS])
        of_tile = sb("of_tile", [P, 4])
        table_i = sb("table_i", [1, 2, SLOTS], I32)
        ones_f = sb("ones_f", [P, EXPERTS])

        NX = 4
        rows = [wtok_sb[:].rearrange("p c d -> p (c d)")[:, ROW * i:ROW * (i + 1)] for i in range(NX)]
        rT = [wqkv_sb[:, i, 0:2 * P].rearrange("p (c t) -> p c t", c=2) for i in range(2)]
        row_w, row_id = sb("row_w", [P, NX]), sb("row_id", [P, NX], I32)
        glu, sig = ([q_spread_all[:, i, 4 * b:4 * b + 4, :].rearrange("p a d -> p (a d)")
                     for b in range(2)] for i in range(2))
        lin = [v_sb[:, b, 0:INNER] for b in range(2)]
        act_sb = [p_spread[:, ICH * b:ICH * (b + 1), :].rearrange("p c t -> p (c t)") for b in range(2)]
        aT = [p_spread[:, HEADS // 2 + ICH * b:HEADS // 2 + ICH * (b + 1), :] for b in range(2)]
        y_out = [x_sb[b // 2][:, 2 * (b % 2):2 * (b % 2) + 2, :].rearrange("p c t -> p (c t)")[:, 0:DIM]
                 for b in range(NX)]

        ps_e, ps_p = banks[0][:, 0:DIM], banks[0][:, DIM:2 * DIM]
        ps_cT = banks[0][0:EXPERTS, 2 * DIM:2 * DIM + P]
        ps_qk = banks[1][:, 0:2 * DIM]

        def turned(b, a, rows=HALF):
            return banks[b][0:rows, a:a + 2 * P].rearrange("p (c t) -> p c t", c=2)

        ps_yT = banks[2][:, 0:YCH * P].rearrange("p (c t) -> p c t", c=YCH)
        ps_r, ps_cnt = banks[2][:, 384:384 + EXPERTS], banks[2][:, 416:416 + EXPERTS]
        ps_qT, ps_b = turned(3, 0), banks[3][:, 256:256 + DIM]
        ps_kT, ps_g = turned(4, 0), banks[4][:, 256:256 + EXPERTS]
        ps_pT = banks[5][:, 0:DIM]
        ps_xT, ps_tT = turned(6, 0), turned(6, 256)
        ps_v = banks[7][:, 256:256 + DIM]
        ps_s = banks[7][0:HALF, 0:2 * IMGS * SEQ].rearrange("p (c k) -> p c k", k=SEQ)
        ps_tab = banks[3][0:1, 0:2 * SLOTS]
        ps_glu, ps_lin = [banks[0], banks[1]], [banks[2], banks[3]]
        ps_rT, ps_aT, ps_yo = turned(4, 0), [banks[5], banks[6]], banks[7][:, 0:DIM]

        consts_in, wtok_in, wqkv_in, wsmall_in = sem("consts_in"), sem("wtok_in"), sem("wqkv_in"), sem("wsmall_in")
        x_in = [sem("x_in0"), sem("x_in1")]
        experts_in, base_out, dump_out = sem("experts_in"), sem("base_out"), sem("dump_out")
        setup_pool, setup_dve, setup_act, pad_done = sem("setup_pool"), sem("setup_dve"), sem("setup_act"), sem("pad_done")
        names = ("embedded h0_ready stats1_ready mv1_ready ve1_ready rstd1_ready xn_ready xn_turned xnT_ready "
                 "qk_done v_done rope_c_ready rope_s_ready qk_ready v_ready q_turned k_turned kT_ready q_spread_ready scores_done "
                 "sc1_ready rmax_ready sc2_ready prob_ready rsum_ready rinv_ready probn_ready p_turned "
                 "p_spread_ready pv_done yT_ready proj_done h1_ready stats2_ready mv2_ready "
                 "ve2_ready rstd2_ready x2_ready base_ready ssq_ready msq_ready rms_ready t_row_ready t_turned packed "
                 "tT_ready gated top_v_ready top_i_ready top_f_ready top_d_ready top_e_ready einv_ready top_w_ready "
                 "onehot_ready onehot_w_ready comb_ready weights_ready token_ready chosen_ready ranked comb_turned "
                 "combT_ready b2_done base_full place_ready onehot_r_ready row_f_ready row_i_ready "
                 "chosen_before_ready").split()
        s = {n: sem(n) for n in names}
        scattered = [sem("scattered0"), sem("scattered1")]
        counted, table_step, fill_ready, table_turned, table_ready, spare_out = (
            sem(n) for n in ("counted", "table_step", "fill_ready", "table_turned", "table_ready", "spare_out"))
        pads_out = [sem(f"pads_out{i}") for i in range(3)]
        rows_in = [sem(f"rows_in{i}") for i in range(NX)]
        r_names = ("rows_turned rT_ready glu_done lin_done glu_ready sig_ready lin_ready gl_ready act_ready "
                   "act_turned aT_ready experts_done y_out_ready noted added").split()
        r = {n: sem("r_" + n) for n in r_names}

        def wait(eng, semaphore, count):
            if not (isinstance(count, int) and count <= 0):
                eng.wait_ge(semaphore, count)

        def rows_out(t, buf):
            return (t - buf) * 8 * TOPK

        def alone(eng):
            eng.nop(nofuse=True)

        def pipeline(eng, stages, tiles, step, unroll):
            first = -(-stages // unroll) * unroll
            last = first + (tiles - first) // unroll * unroll

            def written_out(n):
                step(lambda k: n - k if 0 <= n - k < tiles else None,
                     lambda k, back=0: min(max(n - back - k + 1, 0), tiles), n)

            for n in range(first):
                written_out(n)
            with eng.Fori(first, last - unroll + 1, unroll) as n0:
                for u in range(unroll):
                    step(lambda k: n0 + (u - k), lambda k, back=0: n0 + (u - k + 1 - back), u)
            for n in range(last, tiles + stages - 1):
                written_out(n)

        def pad_regions(eng, i):
            eng.wait_ge(fill_ready, 1)
            with eng.Fori(PAD_SPLIT[i], PAD_SPLIT[i + 1] - 1, 2) as e0:
                for u in range(2):
                    at = eng.value_load(fill_i[0:1, bass.ds(e0 + u, 1)], min_val=0, max_val=SPARE - P)
                    eng.dma_start(routed[bass.ds(at, P), :], pad_row[:]).then_inc(pads_out[i], 16)

        block = ctx.enter_context(nc.Block())

        @block.sync
        def _(sp):
            sp.dma_start(x_sb[0][:], x[0]).then_inc(x_in[0], 16)
            sp.dma_start(wtok_sb[:], w_tok).then_inc(wtok_in, 16)
            sp.dma_start(cst[:], consts).then_inc(consts_in, 16)
            sp.dma_start(btok_bc[:], b_tok.to_broadcast([P, DIM])).then_inc(wsmall_in, 16)
            sp.dma_start(wqkv_sb[0:HALF], w_qkv).then_inc(wqkv_in, 16)
            sp.dma_start(wqkv_sb[HALF:HALF + 1, 1, :], b_qkv).then_inc(wqkv_in, 16)
            sp.dma_start(wproj_sb[:], w_proj).then_inc(wsmall_in, 16)
            sp.dma_start(nscale_bc[:], nscale.to_broadcast([P, DIM])).then_inc(wsmall_in, 16)
            sp.dma_start(wgate_sb[0:HALF], w_gate).then_inc(wsmall_in, 16)
            sp.dma_start(wgate_sb[HALF:HALF + 1, 1, :], b_gate).then_inc(wsmall_in, 16)
            sp.dma_start(b2_sb[:], b2).then_inc(wsmall_in, 16)

            def load_x(t, buf):
                wait(sp, s["embedded"], t - 1)
                sp.dma_start(x_sb[buf][:], x[bass.ds(t, 1)].rearrange("a p c t -> (a p) c t")
                             ).then_inc(x_in[buf], 16)

            def load_expert(e):
                sp.dma_start(w1_sb[0:HALF, :, bass.ds(e, 1), :], w1[:, :, bass.ds(e, 1), :]).then_inc(experts_in, 16)
                sp.dma_start(w1_sb[HALF:HALF + 1, 1, bass.ds(e, 1), :], b1[:, bass.ds(e, 1), :]).then_inc(experts_in, 16)
                sp.dma_start(w2_sb[:, bass.ds(e, 1)], w2[:, bass.ds(e, 1)]).then_inc(experts_in, 16)

            def store_base(t):
                wait(sp, s["base_full"], t + 1)
                sp.dma_start(out[bass.ds(t * P, P), :], base[:, bass.ds(t, 1), :].rearrange("p a d -> p (a d)")
                             ).then_inc(base_out, 16)

            load_x(1, 1)
            load_expert(0)
            for t in range(2, 8):
                load_x(t, t % 2)
                load_expert(t - 1)
            with sp.Fori(8, TILES - 1, 2) as t0:
                for u in range(2):
                    load_x(t0 + u, u)
                    load_expert(t0 + (u - 1))
                    store_base(t0 + (u - 8))
            load_expert(TILES - 1)
            sp.wait_ge(pad_done, 1)
            sp.dma_start(routed[SPARE:SPARE + P, :], pad_row[:]).then_inc(spare_out, 16)
            sp.dma_start(out[TOKENS:TOKENS + P, :], pad_row[:, 0:DIM]).then_inc(dump_out, 16)
            with sp.Fori(TILES - 8, TILES) as t:
                store_base(t)
            pad_regions(sp, 0)
            sp.wait_ge(spare_out, 16)
            for i in range(3):
                sp.wait_ge(pads_out[i], 16 * (PAD_SPLIT[i + 1] - PAD_SPLIT[i]))
            for buf in range(2):
                sp.wait_ge(scattered[buf], 16 * TOPK * TILES // 2)
            sp.wait_ge(table_ready, 1)

            def load_rows(j, buf):
                wait(sp, r["rows_turned"], j - NX + 1)
                alone(sp)
                wait(sp, r["noted"], 2 * (j - NX + 1))
                alone(sp)
                at = sp.value_load(table_i[0:1, 1, bass.ds(j, 1)], min_val=0, max_val=SPARE)
                sp.dma_start(rows[buf], routed[bass.ds(at, P), :]).then_inc(rows_in[buf], 16)

            for j in range(NX):
                load_rows(j, j)
            with sp.Fori(NX, SLOTS - NX + 1, NX) as j0:
                for u in range(NX):
                    load_rows(j0 + u, u)
            for j in range(SLOTS // NX * NX, SLOTS):
                load_rows(j, j % NX)
            sp.wait_ge(r["added"], 16 * SLOTS)
            sp.wait_ge(base_out, 16 * TILES)

        @block.tensor
        def _(pe):
            mm, turn = nc.tensor.matmul, nc.tensor.transpose

            def bank_free(*owed):
                for name, count in owed:
                    wait(pe, s[name], count)

            def embed(t, buf, loads):
                pe.wait_ge(x_in[buf], loads)
                for c in range(PCH):
                    last = mm(ps_e, x_sb[buf][:, c, :], wtok_sb[:, c, :], start=(c == 0), stop=(c == PCH - 1))
                last.then_inc(s["embedded"], 1)

            def turn_halves(t, dst, src, ready, done):
                pe.wait_ge(s[ready], t + 1)
                for c in range(2):
                    last = turn(dst[:, c, :], src[:, c * HALF:(c + 1) * HALF], ident)
                last.then_inc(s[done], 1)

            def turn_probs(t):
                pe.wait_ge(s["probn_ready"], t + 1)
                for c in range(2):
                    last = turn(ps_pT[:, c * HALF:(c + 1) * HALF],
                                probn[:, c * IMGS:(c + 1) * IMGS, :].rearrange("p i k -> p (i k)"),
                                ident[0:HALF, 0:HALF])
                last.then_inc(s["p_turned"], 1)

            def rank(t):
                pe.wait_ge(s["chosen_ready"], t + 1)
                pe.wait_ge(s["chosen_before_ready"], t + 1)
                mm(ps_r, before_bf[:], chosen[:], start=True, stop=False)
                mm(ps_r, ones_bf[:], chosen_before[:], start=False, stop=True).then_inc(s["ranked"], 1)

            def turn_weights(t):
                pe.wait_ge(s["comb_ready"], t + 1)
                turn(ps_cT, comb[:], ident).then_inc(s["comb_turned"], 1)

            def qk_product(t):
                pe.wait_ge(s["xnT_ready"], t + 1)
                mm(ps_qk, xnT[0:HALF, 0, :], wqkv_sb[0:HALF, 0, 0:2 * DIM], start=True, stop=False)
                mm(ps_qk, xnT[:, 1, :], wqkv_sb[:, 1, 0:2 * DIM], start=False, stop=True).then_inc(s["qk_done"], 1)

            def v_product(t):
                mm(ps_v, xnT[0:HALF, 0, :], wqkv_sb[0:HALF, 0, 2 * DIM:], start=True, stop=False)
                mm(ps_v, xnT[:, 1, :], wqkv_sb[:, 1, 2 * DIM:], start=False, stop=True).then_inc(s["v_done"], 1)

            def scores(t):
                pe.wait_ge(s["kT_ready"], t + 1)
                pe.wait_ge(s["q_spread_ready"], t + 1)
                for c in range(2):
                    for i in range(IMGS):
                        last = mm(ps_s[:, c * IMGS + i, :], q_spread[:, c, i, :], kT[:, c, i * SEQ:(i + 1) * SEQ],
                                  start=True, stop=True)
                last.then_inc(s["scores_done"], 1)

            def project(t):
                pe.wait_ge(s["yT_ready"], t + 1)
                for c in range(YCH):
                    last = mm(ps_p, yT[:, c, :], wproj_sb[:, c, :], start=(c == 0), stop=(c == YCH - 1))
                last.then_inc(s["proj_done"], 1)

            def gate(t):
                pe.wait_ge(s["tT_ready"], t + 1)
                mm(ps_g, tT[0:HALF, 0, :], wgate_sb[0:HALF, 0, :], start=True, stop=False)
                mm(ps_g, tT[:, 1, :], wgate_sb[:, 1, :], start=False, stop=True).then_inc(s["gated"], 1)

            def experts_bias(t):
                pe.wait_ge(s["combT_ready"], t + 1)
                mm(ps_b, combT[:], b2_sb[:], start=True, stop=True).then_inc(s["b2_done"], 1)

            def values(t, buf):
                pe.wait_ge(s["p_spread_ready"], t + 1)
                for h in range(HEADS):
                    g, c = h % (P // GROUP), h // (P // GROUP)
                    last = mm(ps_yT[g * GROUP:(g + 1) * GROUP, c, :], v_sb[:, buf, h * HD:(h + 2) * HD],
                              p_spread[:, h, :], start=True, stop=True)
                last.then_inc(s["pv_done"], 1)

            pe.wait_ge(wtok_in, 16)

            def step(tile, seen, n):
                par = n % 2
                if tile(0) is not None:
                    t = tile(0)
                    bank_free(("h0_ready", seen(0, 1)), ("combT_ready", seen(6, 1)), ("h1_ready", seen(4, 1)))
                    embed(t, par, 16 * (t // 2 + 1) if isinstance(t, int) else (t - par) * 8 + 16)
                if isinstance(tile(0), int) and tile(0) == 0:
                    pe.wait_ge(consts_in, 16)
                    pe.wait_ge(wqkv_in, 32)
                    pe.wait_ge(wsmall_in, 16 * 6)
                    pe.wait_ge(setup_pool, 3)
                    pe.wait_ge(setup_act, 2)
                    pe.wait_ge(setup_dve, 2)
                if tile(1) is not None:
                    bank_free(("xnT_ready", seen(1, 1)), ("tT_ready", seen(5, 1)))
                    turn_halves(tile(1), ps_xT, xn, "xn_ready", "xn_turned")
                if tile(2) is not None:
                    bank_free(("q_spread_ready", seen(2, 1)), ("base_full", seen(6, 1)))
                    turn_halves(tile(2), ps_qT, qk[:, 0:DIM], "qk_ready", "q_turned")
                    bank_free(("kT_ready", seen(2, 1)), ("top_i_ready", seen(5, 1)))
                    turn_halves(tile(2), ps_kT, qk[:, DIM:2 * DIM], "qk_ready", "k_turned")
                if tile(3) is not None:
                    bank_free(("p_spread_ready", seen(3, 1)))
                    turn_probs(tile(3))
                if tile(4) is not None:
                    bank_free(("h1_ready", seen(4, 1)), ("combT_ready", seen(6, 1)), ("h0_ready", seen(0)))
                    project(tile(4))
                if tile(6) is not None:
                    bank_free(("place_ready", seen(6, 1)), ("yT_ready", seen(3, 1)))
                    rank(tile(6))
                if tile(5) is not None:
                    bank_free(("tT_ready", seen(5, 1)), ("xnT_ready", seen(1)))
                    turn_halves(tile(5), ps_tT, t_row[(n - 5) % 2], "t_row_ready", "t_turned")
                if tile(1) is not None:
                    bank_free(("rope_s_ready", seen(1, 1)))
                    qk_product(tile(1))
                if tile(6) is not None:
                    bank_free(("combT_ready", seen(6, 1)), ("h0_ready", seen(0)), ("h1_ready", seen(4)))
                    turn_weights(tile(6))
                if tile(5) is not None:
                    bank_free(("top_i_ready", seen(5, 1)), ("kT_ready", seen(2)))
                    gate(tile(5))
                if tile(2) is not None:
                    bank_free(("sc1_ready", seen(2, 1)), ("v_ready", seen(1, 1)))
                    scores(tile(2))
                if isinstance(tile(6), int) and tile(6) == TILES - 1:
                    pe.wait_ge(s["place_ready"], TILES)
                    pe.wait_ge(s["chosen_before_ready"], TILES + 1)
                    mm(ps_cnt, ones_bf[:], chosen_before[:], start=True, stop=True).then_inc(counted, 1)
                if tile(6) is not None:
                    bank_free(("base_full", seen(6, 1)), ("q_spread_ready", seen(2)))
                    experts_bias(tile(6))
                if tile(3) is not None:
                    bank_free(("yT_ready", seen(3, 1)), ("place_ready", seen(6)))
                    values(tile(3), (n - 3) % 2)
                if tile(1) is not None:
                    bank_free(("v_ready", seen(1, 1)), ("sc1_ready", seen(2)))
                    v_product(tile(1))

            pipeline(pe, STAGES, TILES, step, 2)

            pe.wait_ge(s["base_full"], TILES)
            pe.wait_ge(table_step, TABLE_STEPS)
            for i in range(2):
                last = mm(ps_tab[:, i * SLOTS:(i + 1) * SLOTS], of_tile[0:SLOTS, i:i + 1], ident[0:SLOTS, 0:SLOTS],
                          start=True, stop=True)
            last.then_inc(table_turned, 1)

            pe.wait_ge(table_ready, 1)
            pe.wait_ge(setup_dve, 4)
            pe.wait_ge(experts_in, 16 * 3 * EXPERTS)
            pe.wait_ge(s["base_full"], TILES)
            pe.wait_ge(s["row_i_ready"], TILES)

            def turn_rows(j, buf, count):
                pe.wait_ge(rows_in[buf], count)
                wait(pe, r["rT_ready"], j)
                for c in range(2):
                    last = turn(ps_rT[:, c, :], rows[buf][:, c * HALF:(c + 1) * HALF], ident)
                last.then_inc(r["rows_turned"], 1)

            def first_layer(j, buf, expert, part, dst, free, done):
                wait(pe, r[free], j - 1)
                a = part * INNER
                for c, k in ((0, HALF), (1, HALF + 1)):
                    last = mm(dst[buf % 2][:, 0:INNER], rT[buf % 2][0:k, c, :],
                              w1_sb[0:k, c, bass.ds(expert, 1), a:a + INNER].rearrange("p a f -> p (a f)"),
                              start=(c == 0), stop=(c == 1))
                last.then_inc(r[done], 1)

            def turn_act(j, buf):
                pe.wait_ge(r["act_ready"], j + 1)
                wait(pe, r["aT_ready"], j - 1)
                for c in range(ICH):
                    last = turn(ps_aT[buf % 2][:, c * P:(c + 1) * P], act_sb[buf % 2][:, c * P:(c + 1) * P], ident)
                last.then_inc(r["act_turned"], 1)

            def second_layer(j, buf, expert):
                pe.wait_ge(r["aT_ready"], j + 1)
                wait(pe, r["y_out_ready"], j)
                for c in range(ICH):
                    last = mm(ps_yo, aT[buf % 2][:, c, :],
                              w2_sb[:, bass.ds(expert, 1), c, :].rearrange("p a f -> p (a f)"),
                              start=(c == 0), stop=(c == ICH - 1))
                last.then_inc(r["experts_done"], 1)

            def expert_of(j):
                return pe.value_load(table_i[0:1, 0, bass.ds(j, 1)], min_val=0, max_val=EXPERTS - 1)

            held = {}

            def r_step(tile, seen, n):
                b0, b1_, b2_ = n % NX, (n - 1) % NX, (n - 2) % NX
                if n == 0:
                    held.clear()

                def hold(back):
                    if tile(back) is not None and n - back not in held:
                        held[n - back] = expert_of(tile(back))

                hold(1)
                if tile(1) is not None:
                    pe.wait_ge(r["rT_ready"], tile(1) + 1)
                    first_layer(tile(1), b1_, held[n - 1], 0, ps_glu, "glu_ready", "glu_done")
                hold(2)
                if tile(2) is not None:
                    turn_act(tile(2), b2_)
                if tile(0) is not None:
                    j = tile(0)
                    turn_rows(j, b0, 16 * (j // NX + 1) if isinstance(j, int) else (j - b0) * 4 + 16)
                if tile(1) is not None:
                    first_layer(tile(1), b1_, held[n - 1], 1, ps_lin, "lin_ready", "lin_done")
                if tile(0) is not None and (isinstance(tile(0), int) or n < NX - 1):
                    held[n] = expert_of(tile(0))
                if tile(2) is not None:
                    second_layer(tile(2), b2_, held[n - 2])

            pipeline(pe, R_STAGES, SLOTS, r_step, NX)

        @block.scalar
        def _(act):
            def copy(dst, src):
                return nc.scalar.activation(dst, src, ACT.Copy)

            for tile_T in (xnT, tT):
                act.wait_ge(setup_pool, 1)
                copy(tile_T[HALF:HALF + 1, 1, :], ones_bf[HALF:HALF + 1, :]).then_inc(setup_act, 1)

            def move(t, dst, src, done, free, ready):
                act.wait_ge(s[done], t + 1)
                wait(act, s[free], t)
                copy(dst, src).then_inc(s[ready], 1)

            def spread_queries(t):
                act.wait_ge(s["q_turned"], t + 1)
                wait(act, s["scores_done"], t)
                for h in range(HH):
                    last = nc.scalar.activation(
                        q_spread[:, :, :, h * SEQ:(h + 1) * SEQ], ps_qT.rearrange("p c (i q) -> p c i q", q=SEQ),
                        ACT.Copy, scale=const("head", HALF)[:, h:h + 1])
                last.then_inc(s["q_spread_ready"], 1)

            def spread_probs(t):
                act.wait_ge(s["p_turned"], t + 1)
                wait(act, s["pv_done"], t)
                for i in range(IMGS):
                    last = nc.scalar.activation(
                        p_spread[:, :, i * SEQ:(i + 1) * SEQ], ps_pT.rearrange("p (h q) -> p h q", q=SEQ),
                        ACT.Copy, scale=const("image")[:, i:i + 1])
                last.then_inc(s["p_spread_ready"], 1)

            def step(tile, seen, n):
                if tile(6) is not None:
                    t, buf = tile(6), (n - 6) % 2
                    act.wait_ge(s["t_row_ready"], t + 1)
                    wait(act, scattered[buf], rows_out(t, buf))
                    copy(packet[buf][:, 0:DIM], t_row[buf][:]).then_inc(s["packed"], 1)
                if tile(1) is not None:
                    move(tile(1), xnT[0:HALF], ps_xT, "xn_turned", "v_done", "xnT_ready")
                if tile(2) is not None:
                    spread_queries(tile(2))
                if tile(5) is not None:
                    move(tile(5), tT[0:HALF], ps_tT, "t_turned", "gated", "tT_ready")
                if tile(2) is not None:
                    move(tile(2), kT[:], ps_kT, "k_turned", "scores_done", "kT_ready")
                if tile(3) is not None:
                    spread_probs(tile(3))
                if tile(6) is not None:
                    move(tile(6), combT[:], ps_cT, "comb_turned", "b2_done", "combT_ready")
                if tile(4) is not None:
                    t = tile(4)
                    act.wait_ge(s["x2_ready"], t + 1)
                    wait(act, s["msq_ready"], t)
                    nc.scalar.activation(x2sq[:], x2[:], ACT.Square, accum_out=ssq[:]).then_inc(s["ssq_ready"], 1)
                if tile(2) is not None:
                    t = tile(2)
                    act.wait_ge(s["sc2_ready"], t + 1)
                    wait(act, s["probn_ready"], t)
                    wait(act, s["rsum_ready"], t)
                    nc.scalar.activation(prob[:], sc2[:], ACT.Exp).then_inc(s["prob_ready"], 1)
                if tile(5) is not None:
                    t = tile(5)
                    act.wait_ge(s["top_d_ready"], t + 1)
                    wait(act, s["top_w_ready"], t)
                    nc.scalar.activation(top_e[:], top_d[:], ACT.Exp, accum_out=esum[:]).then_inc(s["top_e_ready"], 1)
                if tile(3) is not None:
                    move(tile(3), yT[:], ps_yT, "pv_done", "proj_done", "yT_ready")
                if tile(1) is not None:
                    t = tile(1)
                    act.wait_ge(s["v_done"], t + 1)
                    wait(act, s["pv_done"], t - 1)
                    copy(v_sb[:, (n - 1) % 2, 0:DIM], ps_v).then_inc(s["v_ready"], 1)

            pipeline(act, STAGES, TILES, step, 2)
            pad_regions(act, 1)

            def r_step(tile, seen, n):
                if tile(2) is not None:
                    j, b = tile(2), n % 2
                    act.wait_ge(r["act_turned"], j + 1)
                    wait(act, r["experts_done"], j - 1)
                    copy(aT[b].rearrange("p c t -> p (c t)"), ps_aT[b][:, 0:INNER]).then_inc(r["aT_ready"], 1)
                if tile(0) is not None:
                    j, b = tile(0), n % 2
                    act.wait_ge(r["rows_turned"], j + 1)
                    wait(act, r["lin_done"], j - 1)
                    copy(rT[b][0:HALF], ps_rT).then_inc(r["rT_ready"], 1)
                if tile(1) is not None:
                    j, b = tile(1), (n - 1) % 2
                    act.wait_ge(r["glu_ready"], j + 1)
                    wait(act, r["act_ready"], j - 1)
                    nc.scalar.activation(sig[b], glu[b], ACT.Sigmoid, scale=ALPHA).then_inc(r["sig_ready"], 1)

            pipeline(act, R_STAGES, SLOTS, r_step, NX)

        @block.vector
        def _(dve):
            V = nc.vector
            V.memset(chosen_before[:], 0.0).then_inc(s["chosen_before_ready"], 1)
            dve.wait_ge(consts_in, 16)
            V.tensor_copy(before_bf[:], const("before")).then_inc(setup_dve, 1)
            V.tensor_copy(token_i[:], const("token")).then_inc(setup_dve, 1)
            dve.wait_ge(setup_pool, 2)
            V.tensor_copy(pad_row[:, ID_AT:ID_AT + 1].bitcast(I32), const("pad")).then_inc(pad_done, 1)
            dve.wait_ge(setup_pool, 3)
            dve.wait_ge(wsmall_in, 16 * 6)

            def embed_norm(t):
                dve.wait_ge(s["embedded"], t + 1)
                ht = h0[:, bass.ds(t, 1), :].rearrange("p a d -> p (a d)")
                V.tensor_tensor(ht, ps_e, btok_bc[:], ALU.add).then_inc(s["h0_ready"], 1)
                dve.wait_ge(s["h0_ready"], t + 1)
                alone(dve)
                V.bn_stats(stats1[:], ht).then_inc(s["stats1_ready"], 1)
                dve.wait_ge(s["stats1_ready"], t + 1)
                alone(dve)
                V.bn_aggr(mv1[:], stats1[:]).then_inc(s["mv1_ready"], 1)

            def norm(t):
                ht = h0[:, bass.ds(t, 1), :].rearrange("p a d -> p (a d)")
                dve.wait_ge(s["rstd1_ready"], t + 1)
                wait(dve, s["xn_turned"], t)
                V.tensor_scalar(xn[:], ht, mv1[:, 0:1], rstd1[:], ALU.subtract, ALU.mult).then_inc(s["xn_ready"], 1)

            def rope(t):
                dve.wait_ge(s["qk_done"], t + 1)
                view = ps_qk.rearrange("p (h f u) -> p h f u", h=2 * HEADS, u=2)
                cos = const("cos").unsqueeze(1).to_broadcast([P, 2 * HEADS, HD])
                sin = const("sin").rearrange("p (f u) -> p f u", u=2).unsqueeze(1).to_broadcast(
                    [P, 2 * HEADS, HD // 2, 2])
                V.tensor_tensor(rope_c[:].rearrange("p (h d) -> p h d", d=HD),
                                ps_qk.rearrange("p (h d) -> p h d", d=HD), cos, ALU.mult
                                ).then_inc(s["rope_c_ready"], 1)
                V.tensor_tensor(rope_s[:].rearrange("p (h f u) -> p h f u", h=2 * HEADS, u=2),
                                view[:, :, :, ::-1], sin, ALU.mult).then_inc(s["rope_s_ready"], 1)
                dve.wait_ge(s["rope_s_ready"], t + 1)
                wait(dve, s["k_turned"], t)
                V.tensor_tensor(qk[:], rope_c[:], rope_s[:], ALU.add).then_inc(s["qk_ready"], 1)

            def softmax_top(t):
                dve.wait_ge(s["scores_done"], t + 1)
                causal = const("causal", HALF).unsqueeze(1).to_broadcast([HALF, 2 * IMGS, SEQ])
                V.scalar_tensor_tensor(sc1[:], ps_s, HD ** -0.5, causal, ALU.mult, ALU.add
                                       ).then_inc(s["sc1_ready"], 1)
                dve.wait_ge(s["sc1_ready"], t + 1)
                V.tensor_reduce(rmax[:], sc1[:], AX_X, ALU.max).then_inc(s["rmax_ready"], 1)
                dve.wait_ge(s["rmax_ready"], t + 1)
                wait(dve, s["prob_ready"], t)
                V.tensor_tensor(sc2[:], sc1[:], rmax[:].unsqueeze(2).to_broadcast([HALF, 2 * IMGS, SEQ]),
                                ALU.subtract).then_inc(s["sc2_ready"], 1)

            def softmax_sum(t):
                dve.wait_ge(s["prob_ready"], t + 1)
                V.tensor_reduce(rsum[:], prob[:], AX_X, ALU.add).then_inc(s["rsum_ready"], 1)
                dve.wait_ge(s["rsum_ready"], t + 1)
                wait(dve, s["probn_ready"], t)
                V.reciprocal(rinv[:], rsum[:]).then_inc(s["rinv_ready"], 1)

            def attn_out(t):
                dve.wait_ge(s["proj_done"], t + 1)
                wait(dve, s["base_ready"], t)
                ht = h0[:, bass.ds(t, 1), :].rearrange("p a d -> p (a d)")
                V.tensor_tensor(h1[:], ps_p, ht, ALU.add).then_inc(s["h1_ready"], 1)
                dve.wait_ge(s["h1_ready"], t + 1)
                alone(dve)
                V.bn_stats(stats2[:], h1[:]).then_inc(s["stats2_ready"], 1)
                dve.wait_ge(s["stats2_ready"], t + 1)
                alone(dve)
                V.bn_aggr(mv2[:], stats2[:]).then_inc(s["mv2_ready"], 1)

            def norm2(t):
                dve.wait_ge(s["rstd2_ready"], t + 1)
                wait(dve, s["ssq_ready"], t)
                V.tensor_scalar(x2[:], h1[:], mv2[:, 0:1], rstd2[:], ALU.subtract, ALU.mult
                                ).then_inc(s["x2_ready"], 1)

            def norm3(t, buf):
                dve.wait_ge(s["rms_ready"], t + 1)
                dve.wait_ge(s["x2_ready"], t + 1)
                wait(dve, s["t_turned"], t - 1)
                wait(dve, s["packed"], t - 1)
                V.scalar_tensor_tensor(t_row[buf][:], x2[:], rms[:], nscale_bc[:], ALU.mult, ALU.mult
                                       ).then_inc(s["t_row_ready"], 1)

            def top_experts(t):
                dve.wait_ge(s["gated"], t + 1)
                alone(dve)
                V.max(top_v[:], ps_g).then_inc(s["top_v_ready"], 1)
                dve.wait_ge(s["top_v_ready"], t + 1)
                alone(dve)
                V.max_index(top_i[:], top_v[:], ps_g).then_inc(s["top_i_ready"], 1)
                wait(dve, s["top_e_ready"], t)
                V.tensor_scalar(top_d[:], top_v[:, 0:TOPK], top_v[:, 0:1], None, ALU.subtract
                                ).then_inc(s["top_d_ready"], 1)
                dve.wait_ge(s["top_i_ready"], t + 1)
                V.tensor_copy(top_f[:], top_i[:, 0:TOPK]).then_inc(s["top_f_ready"], 1)

            def weigh_experts(t, buf):
                pke = [P, TOPK, EXPERTS]
                dve.wait_ge(s["top_f_ready"], t + 1)
                V.tensor_tensor(onehot[:], const("expert").unsqueeze(1).to_broadcast(pke),
                                top_f[:].unsqueeze(2).to_broadcast(pke), ALU.is_equal
                                ).then_inc(s["onehot_ready"], 1)
                dve.wait_ge(s["top_e_ready"], t + 1)
                V.reciprocal(einv[:], esum[:]).then_inc(s["einv_ready"], 1)
                dve.wait_ge(s["onehot_ready"], t + 1)
                wait(dve, s["ranked"], t)
                with nc.allow_low_precision("counts of zero or one are exact"):
                    V.tensor_reduce(chosen[:], onehot[:].rearrange("p k e -> p e k"), AX_X, ALU.add
                                    ).then_inc(s["chosen_ready"], 1)
                dve.wait_ge(s["einv_ready"], t + 1)
                V.tensor_scalar(top_w[:], top_e[:], einv[:], None, ALU.mult).then_inc(s["top_w_ready"], 1)
                dve.wait_ge(s["top_w_ready"], t + 1)
                V.tensor_tensor(onehot_w[:], onehot[:], top_w[:].unsqueeze(2).to_broadcast(pke), ALU.mult
                                ).then_inc(s["onehot_w_ready"], 1)
                dve.wait_ge(s["onehot_w_ready"], t + 1)
                wait(dve, s["comb_turned"], t)
                V.tensor_reduce(comb[:], onehot_w[:].rearrange("p k e -> p e k"), AX_X, ALU.add
                                ).then_inc(s["comb_ready"], 1)
                dve.wait_ge(s["comb_ready"], t + 1)
                wait(dve, scattered[buf], rows_out(t, buf))
                V.tensor_copy(packet[buf][:, W_AT:W_AT + EXPERTS], comb[:]).then_inc(s["weights_ready"], 1)
                V.tensor_copy(packet[buf][:, ID_AT:ID_AT + 1].bitcast(I32), token_i[:, bass.ds(t, 1)]
                              ).then_inc(s["token_ready"], 1)

            def place_rows(t, buf):
                pke = [P, TOPK, EXPERTS]
                dve.wait_ge(s["ranked"], t + 1)
                V.tensor_tensor(place[:], ps_r, const("region"), ALU.add).then_inc(s["place_ready"], 1)
                V.tensor_tensor(chosen_before[:], chosen_before[:], chosen[:], ALU.add
                                ).then_inc(s["chosen_before_ready"], 1)
                dve.wait_ge(s["place_ready"], t + 1)
                V.tensor_tensor(onehot_r[:], onehot[:], place[:].unsqueeze(1).to_broadcast(pke), ALU.mult
                                ).then_inc(s["onehot_r_ready"], 1)
                dve.wait_ge(s["onehot_r_ready"], t + 1)
                V.tensor_reduce(row_f[:], onehot_r[:], AX_X, ALU.add).then_inc(s["row_f_ready"], 1)
                dve.wait_ge(s["row_f_ready"], t + 1)
                wait(dve, scattered[buf], rows_out(t, buf))
                V.tensor_copy(row_i[buf][:], row_f[:]).then_inc(s["row_i_ready"], 1)

            def add_bias(t):
                dve.wait_ge(s["b2_done"], t + 1)
                dve.wait_ge(s["base_ready"], t + 1)
                bt = base[:, bass.ds(t, 1), :].rearrange("p a d -> p (a d)")
                V.tensor_tensor(bt, bt, ps_b, ALU.add).then_inc(s["base_full"], 1)

            def step(tile, seen, n):
                if tile(6) is not None:
                    weigh_experts(tile(6), (n - 6) % 2)
                if tile(5) is not None:
                    norm3(tile(5), (n - 5) % 2)
                if tile(0) is not None:
                    embed_norm(tile(0))
                if tile(4) is not None:
                    attn_out(tile(4))
                if tile(0) is not None:
                    norm(tile(0))
                if tile(6) is not None:
                    place_rows(tile(6), (n - 6) % 2)
                if tile(4) is not None:
                    norm2(tile(4))
                if tile(1) is not None:
                    rope(tile(1))
                if tile(5) is not None:
                    top_experts(tile(5))
                if tile(2) is not None:
                    softmax_top(tile(2))
                if tile(6) is not None:
                    add_bias(tile(6))
                if tile(2) is not None:
                    softmax_sum(tile(2))

            pipeline(dve, STAGES, TILES, step, 2)
            for i in range(2):
                V.tensor_copy(rT[i][HALF:HALF + 1, 1, :], ones_bf[HALF:HALF + 1, :]).then_inc(setup_dve, 1)

            made = [0]

            def then_wait(instruction):
                instruction.then_inc(table_step, 1)
                made[0] += 1
                dve.wait_ge(table_step, made[0])

            dve.wait_ge(counted, 1)
            V.tensor_tensor(fill_i[:], ps_cnt[0:1, :], const("region", 1), ALU.add).then_inc(fill_ready, 1)
            then_wait(V.tensor_scalar(cnt_i[:], ps_cnt, float(P - 1), None, ALU.add))
            then_wait(V.tensor_scalar(cnt_i2[:], cnt_i[:], P.bit_length() - 1, None, ALU.logical_shift_right))
            then_wait(V.tensor_copy(ntile[:], cnt_i2[:]))
            then_wait(V.tensor_tensor_scan(tend[:], ones_f[:], ntile[:], 0.0, ALU.mult, ALU.add))
            then_wait(V.tensor_scalar(jump[:], ntile[:], -float(P), float(REGION), ALU.mult, ALU.add))
            then_wait(V.tensor_scalar(passed[:], tend[:], const("tile"), None, ALU.is_le))
            then_wait(V.tensor_tensor(jumped[:], passed[:], jump[:], ALU.mult))
            then_wait(V.tensor_reduce(of_tile[:, 2:3], passed[:], AX_X, ALU.add))
            then_wait(V.tensor_reduce(of_tile[:, 3:4], jumped[:], AX_X, ALU.add))
            then_wait(V.tensor_scalar(of_tile[:, 0:1], of_tile[:, 2:3], float(EXPERTS - 1), None, ALU.min))
            then_wait(V.scalar_tensor_tensor(of_tile[:, 2:3], const("tile"), float(P), of_tile[:, 3:4],
                                             ALU.mult, ALU.add))
            then_wait(V.tensor_scalar(of_tile[:, 1:2], of_tile[:, 2:3], float(SPARE), None, ALU.min))
            assert made[0] == TABLE_STEPS
            dve.wait_ge(table_turned, 1)
            V.tensor_copy(table_i[:].rearrange("p a j -> p (a j)"), ps_tab).then_inc(table_ready, 1)
            dve.wait_ge(table_ready, 1)

            def r_step(tile, seen, n):
                if tile(1) is not None:
                    j, b = tile(1), (n - 1) % 2
                    dve.wait_ge(r["glu_done"], j + 1)
                    wait(dve, r["sig_ready"], j - 1)
                    V.tensor_scalar(glu[b], ps_glu[b][:, 0:INNER], LIMIT, None, ALU.min
                                    ).then_inc(r["glu_ready"], 1)
                    dve.wait_ge(r["lin_done"], j + 1)
                    V.tensor_scalar(lin[b], ps_lin[b][:, 0:INNER], LIMIT, -LIMIT, ALU.min, ALU.max
                                    ).then_inc(r["lin_ready"], 1)
                    dve.wait_ge(r["lin_ready"], j + 1)
                    V.scalar_tensor_tensor(lin[b], lin[b], 1.0, glu[b], ALU.add, ALU.mult
                                           ).then_inc(r["gl_ready"], 1)
                    dve.wait_ge(r["gl_ready"], j + 1)
                    dve.wait_ge(r["sig_ready"], j + 1)
                    wait(dve, r["act_turned"], j - 1)
                    V.tensor_tensor(act_sb[b], lin[b], sig[b], ALU.mult).then_inc(r["act_ready"], 1)
                if tile(2) is not None:
                    j, b = tile(2), (n - 2) % NX
                    dve.wait_ge(r["experts_done"], j + 1)
                    wait(dve, r["added"], 16 * (j - NX + 2))
                    dve.wait_ge(r["noted"], 2 * (j + 1))
                    V.tensor_scalar(y_out[b], ps_yo, row_w[:, b:b + 1], None, ALU.mult
                                    ).then_inc(r["y_out_ready"], 1)

            pipeline(dve, R_STAGES, SLOTS, r_step, NX)

        @block.gpsimd
        def _(pool):
            G = nc.gpsimd
            G.memset(ones_bf[:], 1.0).then_inc(setup_pool, 1)
            G.memset(pad_row[:], 0.0).then_inc(setup_pool, 1)
            for buf in packet:
                G.memset(buf[:], 0.0)
            G.memset(v_sb[:, :, DIM + 1:V_N], 0.0)
            G.memset(v_sb[:, :, DIM:DIM + 1], 1.0)
            G.memset(power[:], -0.5)
            G.memset(ones_f[:], 1.0).then_inc(setup_pool, 1)
            pool.wait_ge(setup_pool, 3)

            def inverse_root(t, var, scale, ready, tmp, tmp_ready, dst, free, dst_ready):
                pool.wait_ge(s[ready], t + 1)
                alone(pool)
                G.tensor_scalar(tmp[:], var, scale, EPS, ALU.mult, ALU.add).then_inc(s[tmp_ready], 1)
                pool.wait_ge(s[tmp_ready], t + 1)
                wait(pool, s[free], t)
                G.tensor_tensor(dst[:], tmp[:], power[:], ALU.pow).then_inc(s[dst_ready], 1)

            def scatter(t, buf):
                pool.wait_ge(s["row_i_ready"], t + 1)
                pool.wait_ge(s["packed"], t + 1)
                pool.wait_ge(s["weights_ready"], t + 1)
                pool.wait_ge(s["token_ready"], t + 1)
                alone(pool)
                for k in range(TOPK):
                    G.indirect_dma_start(out=routed, out_offset=bass.IndirectOffsetOnAxis(ap=row_i[buf][:, k:k + 1].bitcast(U32), axis=0),
                                         in_=packet[buf][:], in_offset=None).then_inc(scattered[buf], 16)

            def residual(t):
                pool.wait_ge(s["x2_ready"], t + 1)
                G.tensor_tensor(base[:, bass.ds(t, 1), :].rearrange("p a d -> p (a d)"), h1[:], x2[:], ALU.add
                                ).then_inc(s["base_ready"], 1)

            def normalise(t):
                pool.wait_ge(s["rinv_ready"], t + 1)
                wait(pool, s["p_turned"], t)
                G.tensor_tensor(probn[:], prob[:], rinv[:].unsqueeze(2).to_broadcast([HALF, 2 * IMGS, SEQ]),
                                ALU.mult).then_inc(s["probn_ready"], 1)

            def step(tile, seen, n):
                if tile(0) is not None:
                    inverse_root(tile(0), mv1[:, 1:2], 1.0, "mv1_ready", ve1, "ve1_ready", rstd1, "xn_ready",
                                 "rstd1_ready")
                if tile(4) is not None:
                    inverse_root(tile(4), mv2[:, 1:2], 1.0, "mv2_ready", ve2, "ve2_ready", rstd2, "x2_ready",
                                 "rstd2_ready")
                if tile(6) is not None and tile(2) is not None:
                    scatter(tile(6), (n - 6) % 2)
                if tile(4) is not None:
                    inverse_root(tile(4), ssq[:], 1.0 / DIM, "ssq_ready", msq, "msq_ready", rms, "t_row_ready",
                                 "rms_ready")
                    residual(tile(4))
                if tile(2) is not None:
                    normalise(tile(2))
                elif tile(6) is not None:
                    scatter(tile(6), (n - 6) % 2)

            pipeline(pool, STAGES, TILES, step, 2)
            pad_regions(pool, 2)
            pool.wait_ge(base_out, 16 * TILES)
            pool.wait_ge(dump_out, 16)
            pool.wait_ge(table_ready, 1)

            def r_step(tile, seen, n):
                if tile(1) is not None:
                    j, b = tile(1), (n - 1) % NX
                    e = pool.value_load(table_i[0:1, 0, bass.ds(j, 1)], min_val=0, max_val=EXPERTS - 1)
                    pool.wait_ge(rows_in[b], 16 * (j // NX + 1) if isinstance(j, int) else (j - b) * 4 + 16)
                    wait(pool, r["added"], 16 * (j - NX + 1))
                    alone(pool)
                    G.tensor_copy(row_w[:, b:b + 1], rows[b][:, bass.ds(e + W_AT, 1)]).then_inc(r["noted"], 1)
                    G.tensor_copy(row_id[:, b:b + 1], rows[b][:, ID_AT:ID_AT + 1].bitcast(I32)
                                  ).then_inc(r["noted"], 1)
                if tile(2) is not None:
                    j, b = tile(2), (n - 2) % NX
                    pool.wait_ge(r["y_out_ready"], j + 1)
                    wait(pool, r["added"], 16 * j)
                    alone(pool)
                    G.indirect_dma_start(out=out, out_offset=bass.IndirectOffsetOnAxis(
                        ap=row_id[:, b:b + 1].bitcast(U32), axis=0),
                        in_=y_out[b], in_offset=None, compute_op=ALU.add).then_inc(r["added"], 16)

            pipeline(pool, R_STAGES, SLOTS, r_step, NX)


def kernel(x, L0_tok_W, L0_tok_b, L0_attn_W_attn, L0_attn_b_attn, L0_attn_W_proj, L0_attn_b_proj,
           L0_ffn_norm_scale, L0_ffn_gate_w, L0_ffn_gate_b, L0_ffn_mlp1_w, L0_ffn_mlp1_b, L0_ffn_mlp2_w,
           L0_ffn_mlp2_b):
    import concourse.bacc as bacc
    from concourse.bass_utils import run_bass_kernel_spmd

    def lay(a, *shape):
        return np.ascontiguousarray(a).reshape(shape)

    def halves(w):
        return np.ascontiguousarray(np.asarray(w).reshape(2, HALF, -1).transpose(1, 0, 2))

    x = np.asarray(x)
    side, w = 4, 16
    patches = x.reshape(TILES, IMGS, 3, side, w, side, w).transpose(0, 4, 6, 2, 1, 3, 5)
    patches = patches.reshape(TILES, PCH, P, P).transpose(0, 2, 1, 3)
    w_tok = np.asarray(L0_tok_W).T.reshape(PCH, P, DIM).transpose(1, 0, 2)
    w1 = np.asarray(L0_ffn_mlp1_w).reshape(EXPERTS, INNER, 2, 2, HALF).transpose(4, 3, 0, 2, 1)
    b1 = np.asarray(L0_ffn_mlp1_b).reshape(1, EXPERTS, INNER, 2).transpose(0, 1, 3, 2)
    w2 = np.asarray(L0_ffn_mlp2_w).reshape(EXPERTS, DIM, ICH, P).transpose(3, 0, 2, 1)
    w_proj = np.zeros((P // GROUP, GROUP, YCH, DIM), np.float32)
    w_proj[:, 0:HD] = np.asarray(L0_attn_W_proj).reshape(YCH, P // GROUP, HD, DIM).transpose(1, 2, 0, 3)
    w_proj[-1, HD, -1] = np.asarray(L0_attn_b_proj)
    w_proj = w_proj.reshape(P, YCH, DIM)
    arrays = {
        "patches": lay(patches, TILES, P, PCH, P),
        "consts": shape_constants(),
        "w_tok": lay(w_tok, P, PCH, DIM),
        "b_tok": lay(L0_tok_b, 1, DIM),
        "w_qkv": halves(L0_attn_W_attn),
        "b_qkv": lay(L0_attn_b_attn, 1, 3 * DIM),
        "w_proj": w_proj,
        "nscale": lay(L0_ffn_norm_scale, 1, DIM),
        "w_gate": halves(np.asarray(L0_ffn_gate_w).T),
        "b_gate": lay(L0_ffn_gate_b, 1, EXPERTS),
        "w1": lay(w1, HALF, 2, EXPERTS, 2 * INNER),
        "b1": lay(b1, 1, EXPERTS, 2 * INNER),
        "w2": lay(w2, P, EXPERTS, ICH, DIM),
        "b2": lay(L0_ffn_mlp2_b, EXPERTS, DIM),
    }
    nc = bacc.Bacc("TRN2", target_bir_lowering=False, num_devices=1)
    args = [nc.dram_tensor(n, a.shape, F32, kind="ExternalInput").ap() for n, a in arrays.items()]
    out = nc.dram_tensor("out_rows", (TOKENS + P, DIM), F32, kind="ExternalOutput").ap()
    build(nc, *args, out)
    result = run_bass_kernel_spmd(nc, [arrays], core_ids=[0])
    return result.results[0]["out_rows"][:TOKENS].reshape(TILES * IMGS, SEQ, DIM)
```

```python
from contextlib import ExitStack

import numpy as np

import concourse.bass as bass
from concourse import mybir

ALU = mybir.AluOpType
ACT = mybir.ActivationFunctionType
AX_X = mybir.AxisListType.X
F32 = mybir.dt.float32
BF16 = mybir.dt.bfloat16
I32 = mybir.dt.int32
U32 = mybir.dt.uint32

P = 128
TOKENS = 2048
TILES = TOKENS // P
SEQ = 16
IMGS = P // SEQ
DIM = 192
HALF = DIM // 2
PATCH = 768
PCH = PATCH // P
HEADS, HD = 12, 16
HH = HEADS // 2
EXPERTS, TOPK = 16, 4
INNER = 384
ICH = INNER // P
EPS = 1e-5
LIMIT, ALPHA = 7.0, 1.702
NEG = -1e30

REGION = TOKENS + P
SPARE = EXPERTS * REGION
SLOTS = TOKENS * TOPK // P + EXPERTS - 1
ROW = 212
W_AT, ID_AT = DIM, DIM + EXPERTS

PAD_SPLIT = (0, 8, 14, 16)
TABLE_STEPS = 12
GROUP = 32
PAIRS = P // GROUP
YCH = HEADS // (P // GROUP)
V_N = DIM + HD
STAGES = 7
R_STAGES = 3

C_COLS = {}
_at = 0
for _name, _n in (("ident", P), ("cos", HD), ("sin", HD), ("head", HH), ("odd", 2), ("own", 2), ("causal", SEQ),
                  ("expert", EXPERTS), ("region", EXPERTS), ("grow", EXPERTS), ("tile", 1), ("pad", 1),
                  ("before", P), ("token", TILES)):
    C_COLS[_name] = (_at, _at + _n)
    _at += _n
C_N = _at


def shape_constants():
    c = np.zeros((P, C_N), np.float32)

    def put(name, value):
        a, b = C_COLS[name]
        c[:, a:b] = value

    p = np.arange(P)
    inv = (1.0 / np.float32(10000.0) ** (np.arange(0, HD, 2, dtype=np.float32) / np.float32(HD))).astype(np.float32)
    angle = ((p % SEQ).astype(np.float32)[:, None] * inv[None, :]).astype(np.float32)
    put("ident", np.eye(P))
    put("cos", np.repeat(np.cos(angle), 2, axis=1))
    put("sin", np.repeat(np.sin(angle), 2, axis=1) * np.tile([-1.0, 1.0], HD // 2))
    put("head", (p[:, None] // HD) == np.arange(HH)[None, :])
    put("odd", (p[:, None] // SEQ % 2) == np.arange(2)[None, :])
    put("own", ((p[:, None] // SEQ % 2) == np.arange(2)[None, :]) * HD ** -0.5)
    put("causal", np.where(np.arange(SEQ)[None, :] > (p % SEQ)[:, None], NEG, 0.0))
    put("expert", np.arange(EXPERTS)[None, :])
    put("region", np.arange(EXPERTS)[None, :] * REGION)
    put("grow", REGION)
    put("tile", p[:, None])
    put("pad", TOKENS + p[:, None])
    put("before", p[:, None] < p[None, :])
    put("token", p[:, None] + P * np.arange(TILES)[None, :])
    return c


def build(nc, x, consts, w_tok, b_tok, w_qkv, b_qkv, w_proj, nscale, w_gate, b_gate,
          w1, b1, w2, b2, out):
    routed = nc.dram_tensor("routed_rows", (SPARE + P, ROW), F32, kind="Internal").ap()
    with ExitStack() as ctx:
        def sb(name, shape, dt=F32):
            return ctx.enter_context(nc.sbuf_tensor(name, shape, dt))

        def bank(name):
            return ctx.enter_context(nc.psum_tensor(name, [P, 512], F32))

        def sem(name):
            return ctx.enter_context(nc.semaphore(name))

        banks = [bank(f"bank{i}") for i in range(8)]

        cst = sb("cst", [P, C_N])

        def const(name, rows=P):
            a, b = C_COLS[name]
            return cst[0:rows, a:b]

        ident = const("ident")
        w1_sb = sb("w1_sb", [HALF + 1, 2, EXPERTS, 2 * INNER])
        w2_sb = sb("w2_sb", [P, EXPERTS, ICH, DIM])
        wtok_sb = sb("wtok_sb", [P, PCH, DIM])
        wqkv_sb = sb("wqkv_sb", [HALF + 1, 2, 3 * DIM])
        wproj_sb = sb("wproj_sb", [P, YCH, DIM])
        wgate_sb = sb("wgate_sb", [HALF + 1, 2, EXPERTS])
        b2_sb = sb("b2_sb", [EXPERTS, DIM])
        btok_bc = sb("btok_bc", [P, DIM])
        nscale_bc = sb("nscale_bc", [P, DIM])
        power = sb("power", [P, 1])
        ones_bf = sb("ones_bf", [P, P], BF16)
        before_bf = sb("before_bf", [P, P], BF16)
        token_i = sb("token_i", [P, TILES], I32)
        pad_row = sb("pad_row", [P, ROW])
        h0 = sb("h0", [P, TILES, DIM])
        base = h0
        v_sb = sb("v_sb", [P, 2, 2 * DIM])

        x_sb = [sb(f"x_sb{i}", [P, PCH, P]) for i in range(2)]
        stats1, mv1, ve1, rstd1 = sb("stats1", [P, 6]), sb("mv1", [P, 2]), sb("ve1", [P, 1]), sb("rstd1", [P, 1])
        xn = sb("xn", [P, DIM])
        xnT = sb("xnT", [HALF + 1, 2, P])
        rope_c, rope_s = sb("rope_c", [P, 2 * DIM]), sb("rope_s", [P, 2 * DIM])
        qk = sb("qk", [P, 2 * DIM])
        qT = sb("qT", [HALF, 2, P])
        k_spread_all = sb("k_spread", [P, 2, IMGS, HH * SEQ])
        k_spread = k_spread_all[0:HALF].rearrange("p c i (h k) -> p c (i h k)", h=HH).rearrange(
            "p c (j h i k) -> p c j h i k", j=PAIRS, h=HH, i=2)
        half_s, sc1, sc2, prob = (sb(n, [P, HEADS, SEQ]) for n in ("half_s", "sc1", "sc2", "prob"))
        rmax, rsum, rinv = (sb(n, [P, HEADS]) for n in ("rmax", "rsum", "rinv"))
        rinv_own = sb("rinv_own", [P, 2, HEADS])
        p_pair = sb("p_pair", [P, HEADS, 2, SEQ])
        pT = sb("pT", [P, HEADS, GROUP])
        p_spread = sb("p_spread", [P, HEADS, P])
        yT = sb("yT", [P, YCH, P])
        h1 = sb("h1", [P, DIM])
        stats2, mv2, ve2, rstd2 = sb("stats2", [P, 6]), sb("mv2", [P, 2]), sb("ve2", [P, 1]), sb("rstd2", [P, 1])
        x2, x2sq = sb("x2", [P, DIM]), sb("x2sq", [P, DIM])
        ssq, msq, rms = sb("ssq", [P, 1]), sb("msq", [P, 1]), sb("rms", [P, 1])
        t_row = [sb(f"t_row{i}", [P, DIM]) for i in range(2)]
        packet = [sb(f"packet{i}", [P, ROW]) for i in range(2)]
        tT = sb("tT", [HALF + 1, 2, P])
        top_v, top_i, top_f = sb("top_v", [P, 8]), sb("top_i", [P, 8], U32), sb("top_f", [P, TOPK])
        top_d, top_e, top_w = sb("top_d", [P, TOPK]), sb("top_e", [P, TOPK]), sb("top_w", [P, TOPK])
        esum, einv = sb("esum", [P, 1]), sb("einv", [P, 1])
        onehot = sb("onehot", [P, TOPK, EXPERTS])
        onehot_w = sb("onehot_w", [P, TOPK, EXPERTS])
        onehot_r = sb("onehot_r", [P, TOPK, EXPERTS])
        comb = sb("comb", [P, EXPERTS])
        combT = sb("combT", [EXPERTS, P])
        chosen = sb("chosen", [P, EXPERTS], BF16)
        chosen_before = sb("chosen_before", [P, EXPERTS], BF16)
        place = sb("place", [P, EXPERTS])
        row_f = sb("row_f", [P, TOPK])
        row_i = [sb(f"row_i{i}", [P, TOPK], I32) for i in range(2)]

        cnt = sb("cnt", [P, EXPERTS])
        cnt_i, cnt_i2 = sb("cnt_i", [P, EXPERTS], I32), sb("cnt_i2", [P, EXPERTS], I32)
        fill_i = sb("fill_i", [1, EXPERTS], I32)
        ntile, tend = sb("ntile", [P, EXPERTS]), sb("tend", [P, EXPERTS])
        passed, jump, jumped = sb("passed", [P, EXPERTS]), sb("jump", [P, EXPERTS]), sb("jumped", [P, EXPERTS])
        of_tile = sb("of_tile", [P, 4])
        table_i = sb("table_i", [1, 2, SLOTS], I32)
        ones_f = sb("ones_f", [P, EXPERTS])

        NX = 4
        rows = [wtok_sb[:].rearrange("p c d -> p (c d)")[:, ROW * i:ROW * (i + 1)] for i in range(NX)]
        rT = [wqkv_sb[:, i, 0:2 * P].rearrange("p (c t) -> p c t", c=2) for i in range(2)]
        row_w, row_id = sb("row_w", [P, NX]), sb("row_id", [P, NX], I32)
        glu, sig = ([k_spread_all[:, i, 4 * b:4 * b + 4, :].rearrange("p a d -> p (a d)")
                     for b in range(2)] for i in range(2))
        lin = [v_sb[:, b, 0:INNER] for b in range(2)]
        act_sb = [p_spread[:, ICH * b:ICH * (b + 1), :].rearrange("p c t -> p (c t)") for b in range(2)]
        aT = [p_spread[:, HEADS // 2 + ICH * b:HEADS // 2 + ICH * (b + 1), :] for b in range(2)]
        y_out = [x_sb[b // 2][:, 2 * (b % 2):2 * (b % 2) + 2, :].rearrange("p c t -> p (c t)")[:, 0:DIM]
                 for b in range(NX)]

        ps_e, ps_cT = banks[0][:, 0:DIM], banks[0][0:EXPERTS, 256:256 + P]
        ps_qk = banks[1][:, 0:2 * DIM]

        def turned(b, a, rows=HALF):
            return banks[b][0:rows, a:a + 2 * P].rearrange("p (c t) -> p c t", c=2)

        ps_yT = banks[2][:, 0:YCH * P].rearrange("p (c t) -> p c t", c=YCH)
        ps_r, ps_cnt = banks[2][:, 384:384 + EXPERTS], banks[2][:, 416:416 + EXPERTS]
        ps_qT, ps_b = turned(3, 0), banks[3][:, 256:256 + DIM]
        ps_kT, ps_g = turned(4, 0), banks[4][:, 256:256 + EXPERTS]
        ps_v, ps_p = banks[5][:, 0:DIM], banks[5][:, 256:256 + DIM]
        ps_xT, ps_tT = turned(6, 0), turned(6, 256)
        ps_s = banks[7][:, 0:HEADS * GROUP]
        ps_tab = banks[3][0:1, 0:2 * SLOTS]
        ps_glu, ps_lin = [banks[0], banks[1]], [banks[2], banks[3]]
        ps_rT, ps_aT, ps_yo = turned(4, 0), [banks[5], banks[6]], banks[7][:, 0:DIM]

        consts_in, wtok_in, wqkv_in, wsmall_in = sem("consts_in"), sem("wtok_in"), sem("wqkv_in"), sem("wsmall_in")
        x_in = [sem("x_in0"), sem("x_in1")]
        experts_in, base_out, dump_out = sem("experts_in"), sem("base_out"), sem("dump_out")
        setup_pool, setup_dve, setup_act, pad_done = (
            sem(n) for n in ("setup_pool", "setup_dve", "setup_act", "pad_done"))
        names = ("embedded h0_ready stats1_ready mv1_ready ve1_ready rstd1_ready xn_ready xn_turned xnT_ready "
                 "qk_done v_done rope_c_ready rope_s_ready qk_ready v_ready q_turned k_turned qT_ready k_spread_ready scores_done "
                 "half_s_ready sc1_ready rmax_ready sc2_ready prob_ready rsum_ready rinv_done rinv_ready p_pair_ready pT_ready "
                 "p_spread_ready pv_done yT_ready proj_done h1_ready stats2_ready mv2_ready "
                 "ve2_ready rstd2_ready x2_ready base_ready ssq_ready msq_ready rms_ready t_row_ready t_turned packed "
                 "tT_ready gated top_v_ready top_i_ready top_f_ready top_d_ready top_e_ready einv_ready top_w_ready "
                 "onehot_ready onehot_w_ready comb_ready weights_ready token_ready chosen_ready ranked comb_turned "
                 "combT_ready b2_done base_full place_ready onehot_r_ready row_f_ready row_i_ready "
                 "chosen_before_ready").split()
        s = {n: sem(n) for n in names}
        scattered = [sem("scattered0"), sem("scattered1")]
        counted, table_step, fill_ready, table_turned, table_ready, spare_out = (
            sem(n) for n in ("counted", "table_step", "fill_ready", "table_turned", "table_ready", "spare_out"))
        pads_out = [sem(f"pads_out{i}") for i in range(3)]
        rows_in = [sem(f"rows_in{i}") for i in range(NX)]
        r_names = ("rows_turned rT_ready glu_done lin_done glu_ready sig_ready lin_ready gl_ready act_ready "
                   "act_turned aT_ready experts_done y_out_ready noted added").split()
        r = {n: sem("r_" + n) for n in r_names}

        def wait(eng, semaphore, count):
            if not (isinstance(count, int) and count <= 0):
                eng.wait_ge(semaphore, count)

        def rows_out(t, buf):
            return (t - buf) * 8 * TOPK

        def alone(eng):
            eng.nop(nofuse=True)

        def pipeline(eng, stages, tiles, step, unroll):
            first = -(-stages // unroll) * unroll
            last = first + (tiles - first) // unroll * unroll

            def written_out(n):
                step(lambda k: n - k if 0 <= n - k < tiles else None,
                     lambda k, back=0: min(max(n - back - k + 1, 0), tiles), n)

            for n in range(first):
                written_out(n)
            with eng.Fori(first, last - unroll + 1, unroll) as n0:
                for u in range(unroll):
                    step(lambda k: n0 + (u - k), lambda k, back=0: n0 + (u - k + 1 - back), u)
            for n in range(last, tiles + stages - 1):
                written_out(n)

        def pad_regions(eng, i):
            eng.wait_ge(fill_ready, 1)
            with eng.Fori(PAD_SPLIT[i], PAD_SPLIT[i + 1] - 1, 2) as e0:
                for u in range(2):
                    at = eng.value_load(fill_i[0:1, bass.ds(e0 + u, 1)], min_val=0, max_val=SPARE - P)
                    eng.dma_start(routed[bass.ds(at, P), :], pad_row[:]).then_inc(pads_out[i], 16)

        block = ctx.enter_context(nc.Block())

        @block.sync
        def _(sp):
            sp.dma_start(x_sb[0][:], x[0]).then_inc(x_in[0], 16)
            sp.dma_start(wtok_sb[:], w_tok).then_inc(wtok_in, 16)
            sp.dma_start(cst[:], consts).then_inc(consts_in, 16)
            sp.dma_start(btok_bc[:], b_tok.to_broadcast([P, DIM])).then_inc(wsmall_in, 16)
            sp.dma_start(wqkv_sb[0:HALF], w_qkv).then_inc(wqkv_in, 16)
            sp.dma_start(wqkv_sb[HALF:HALF + 1, 1, :], b_qkv).then_inc(wqkv_in, 16)
            sp.dma_start(wproj_sb[:], w_proj).then_inc(wsmall_in, 16)
            sp.dma_start(nscale_bc[:], nscale.to_broadcast([P, DIM])).then_inc(wsmall_in, 16)
            sp.dma_start(wgate_sb[0:HALF], w_gate).then_inc(wsmall_in, 16)
            sp.dma_start(wgate_sb[HALF:HALF + 1, 1, :], b_gate).then_inc(wsmall_in, 16)
            sp.dma_start(b2_sb[:], b2).then_inc(wsmall_in, 16)

            def load_x(t, buf):
                wait(sp, s["embedded"], t - 1)
                sp.dma_start(x_sb[buf][:], x[bass.ds(t, 1)].rearrange("a p c t -> (a p) c t")
                             ).then_inc(x_in[buf], 16)

            def load_expert(e):
                sp.dma_start(w1_sb[0:HALF, :, bass.ds(e, 1), :], w1[:, :, bass.ds(e, 1), :]).then_inc(experts_in, 16)
                sp.dma_start(w1_sb[HALF:HALF + 1, 1, bass.ds(e, 1), :], b1[:, bass.ds(e, 1), :]).then_inc(experts_in, 16)
                sp.dma_start(w2_sb[:, bass.ds(e, 1)], w2[:, bass.ds(e, 1)]).then_inc(experts_in, 16)

            def store_base(t):
                wait(sp, s["base_full"], t + 1)
                sp.dma_start(out[bass.ds(t * P, P), :], base[:, bass.ds(t, 1), :].rearrange("p a d -> p (a d)")
                             ).then_inc(base_out, 16)

            load_x(1, 1)
            load_expert(0)
            for t in range(2, 8):
                load_x(t, t % 2)
                load_expert(t - 1)
            with sp.Fori(8, TILES - 1, 2) as t0:
                for u in range(2):
                    load_x(t0 + u, u)
                    load_expert(t0 + (u - 1))
                    store_base(t0 + (u - 8))
            load_expert(TILES - 1)
            sp.wait_ge(pad_done, 1)
            sp.dma_start(routed[SPARE:SPARE + P, :], pad_row[:]).then_inc(spare_out, 16)
            sp.dma_start(out[TOKENS:TOKENS + P, :], pad_row[:, 0:DIM]).then_inc(dump_out, 16)
            with sp.Fori(TILES - 8, TILES - 1) as t:
                store_base(t)
            pad_regions(sp, 0)
            store_base(TILES - 1)
            sp.wait_ge(spare_out, 16)
            for i in range(3):
                sp.wait_ge(pads_out[i], 16 * (PAD_SPLIT[i + 1] - PAD_SPLIT[i]))
            for buf in range(2):
                sp.wait_ge(scattered[buf], 16 * TOPK * TILES // 2)
            sp.wait_ge(table_ready, 1)

            def load_rows(j, buf):
                wait(sp, r["rows_turned"], j - NX + 1)
                alone(sp)
                wait(sp, r["noted"], 2 * (j - NX + 1))
                alone(sp)
                at = sp.value_load(table_i[0:1, 1, bass.ds(j, 1)], min_val=0, max_val=SPARE)
                sp.dma_start(rows[buf], routed[bass.ds(at, P), :]).then_inc(rows_in[buf], 16)

            for j in range(NX):
                load_rows(j, j)
            with sp.Fori(NX, SLOTS - NX + 1, NX) as j0:
                for u in range(NX):
                    load_rows(j0 + u, u)
            for j in range(SLOTS // NX * NX, SLOTS):
                load_rows(j, j % NX)
            sp.wait_ge(r["added"], 16 * SLOTS)
            sp.wait_ge(base_out, 16 * TILES)

        @block.tensor
        def _(pe):
            mm, turn = nc.tensor.matmul, nc.tensor.transpose

            def bank_free(*owed):
                for name, count in owed:
                    wait(pe, s[name], count)

            def embed(t, buf, loads):
                pe.wait_ge(x_in[buf], loads)
                for c in range(PCH):
                    last = mm(ps_e, x_sb[buf][:, c, :], wtok_sb[:, c, :], start=(c == 0), stop=(c == PCH - 1))
                last.then_inc(s["embedded"], 1)

            def turn_halves(t, dst, src, ready, done):
                pe.wait_ge(s[ready], t + 1)
                for c in range(2):
                    last = turn(dst[:, c, :], src[:, c * HALF:(c + 1) * HALF], ident)
                last.then_inc(s[done], 1)

            def rank(t):
                pe.wait_ge(s["chosen_ready"], t + 1)
                pe.wait_ge(s["chosen_before_ready"], t + 1)
                mm(ps_r, before_bf[:], chosen[:], start=True, stop=False)
                mm(ps_r, ones_bf[:], chosen_before[:], start=False, stop=True).then_inc(s["ranked"], 1)

            def turn_weights(t):
                pe.wait_ge(s["comb_ready"], t + 1)
                turn(ps_cT, comb[:], ident).then_inc(s["comb_turned"], 1)

            def qk_product(t):
                pe.wait_ge(s["xnT_ready"], t + 1)
                mm(ps_qk, xnT[0:HALF, 0, :], wqkv_sb[0:HALF, 0, 0:2 * DIM], start=True, stop=False)
                mm(ps_qk, xnT[:, 1, :], wqkv_sb[:, 1, 0:2 * DIM], start=False, stop=True).then_inc(s["qk_done"], 1)

            def v_product(t):
                mm(ps_v, xnT[0:HALF, 0, :], wqkv_sb[0:HALF, 0, 2 * DIM:], start=True, stop=False)
                mm(ps_v, xnT[:, 1, :], wqkv_sb[:, 1, 2 * DIM:], start=False, stop=True).then_inc(s["v_done"], 1)

            def scores(t):
                pe.wait_ge(s["qT_ready"], t + 1)
                pe.wait_ge(s["k_spread_ready"], t + 1)
                n = HH * GROUP
                for c in range(2):
                    for j in range(PAIRS):
                        a = j * GROUP
                        last = mm(ps_s[a:a + GROUP, c * n:(c + 1) * n], qT[:, c, a:a + GROUP],
                                  k_spread[:, c, j].rearrange("p h i k -> p (h i k)"), start=True, stop=True)
                last.then_inc(s["scores_done"], 1)

            def project(t):
                pe.wait_ge(s["yT_ready"], t + 1)
                for c in range(YCH):
                    last = mm(ps_p, yT[:, c, :], wproj_sb[:, c, :], start=(c == 0), stop=(c == YCH - 1))
                last.then_inc(s["proj_done"], 1)

            def gate(t):
                pe.wait_ge(s["tT_ready"], t + 1)
                mm(ps_g, tT[0:HALF, 0, :], wgate_sb[0:HALF, 0, :], start=True, stop=False)
                mm(ps_g, tT[:, 1, :], wgate_sb[:, 1, :], start=False, stop=True).then_inc(s["gated"], 1)

            def experts_bias(t):
                pe.wait_ge(s["combT_ready"], t + 1)
                mm(ps_b, combT[:], b2_sb[:], start=True, stop=True).then_inc(s["b2_done"], 1)

            def values(t, buf):
                pe.wait_ge(s["p_spread_ready"], t + 1)
                for h in range(HEADS):
                    g, c = h % (P // GROUP), h // (P // GROUP)
                    last = mm(ps_yT[g * GROUP:(g + 1) * GROUP, c, :], v_sb[:, buf, h * HD:(h + 2) * HD],
                              p_spread[:, h, :], start=True, stop=True)
                last.then_inc(s["pv_done"], 1)

            pe.wait_ge(wtok_in, 16)

            def step(tile, seen, n):
                par = n % 2
                if tile(0) is not None:
                    t = tile(0)
                    bank_free(("h0_ready", seen(0, 1)), ("combT_ready", seen(6, 1)))
                    embed(t, par, 16 * (t // 2 + 1) if isinstance(t, int) else (t - par) * 8 + 16)
                if isinstance(tile(0), int) and tile(0) == 0:
                    pe.wait_ge(consts_in, 16)
                    pe.wait_ge(wqkv_in, 32)
                    pe.wait_ge(wsmall_in, 16 * 6)
                    pe.wait_ge(setup_pool, 3)
                    pe.wait_ge(setup_act, 2)
                    pe.wait_ge(setup_dve, 2)
                if tile(1) is not None:
                    bank_free(("xnT_ready", seen(1, 1)), ("tT_ready", seen(5, 1)))
                    turn_halves(tile(1), ps_xT, xn, "xn_ready", "xn_turned")
                if tile(2) is not None:
                    bank_free(("qT_ready", seen(2, 1)), ("base_full", seen(6, 1)))
                    turn_halves(tile(2), ps_qT, qk[:, 0:DIM], "qk_ready", "q_turned")
                    bank_free(("k_spread_ready", seen(2, 1)), ("top_i_ready", seen(5, 1)))
                    turn_halves(tile(2), ps_kT, qk[:, DIM:2 * DIM], "qk_ready", "k_turned")
                if tile(4) is not None:
                    bank_free(("h1_ready", seen(4, 1)), ("v_ready", seen(1, 1)))
                    project(tile(4))
                if tile(6) is not None:
                    bank_free(("place_ready", seen(6, 1)), ("yT_ready", seen(3, 1)))
                    rank(tile(6))
                    if isinstance(tile(6), int) and tile(6) == TILES - 1:
                        mm(ps_cnt, ones_bf[:], chosen[:], start=True, stop=False)
                        mm(ps_cnt, ones_bf[:], chosen_before[:], start=False, stop=True).then_inc(counted, 1)
                if tile(5) is not None:
                    bank_free(("tT_ready", seen(5, 1)), ("xnT_ready", seen(1)))
                    turn_halves(tile(5), ps_tT, t_row[(n - 5) % 2], "t_row_ready", "t_turned")
                if tile(1) is not None:
                    bank_free(("rope_s_ready", seen(1, 1)))
                    qk_product(tile(1))
                if tile(6) is not None:
                    bank_free(("combT_ready", seen(6, 1)), ("h0_ready", seen(0)))
                    turn_weights(tile(6))
                if tile(5) is not None:
                    bank_free(("top_i_ready", seen(5, 1)), ("k_spread_ready", seen(2)))
                    gate(tile(5))
                if tile(2) is not None:
                    bank_free(("sc1_ready", seen(2, 1)))
                    scores(tile(2))
                if tile(3) is not None:
                    bank_free(("yT_ready", seen(3, 1)), ("place_ready", seen(6)))
                    values(tile(3), (n - 3) % 2)
                if tile(6) is not None:
                    bank_free(("base_full", seen(6, 1)), ("qT_ready", seen(2)))
                    experts_bias(tile(6))
                if tile(1) is not None:
                    bank_free(("v_ready", seen(1, 1)), ("h1_ready", seen(4)))
                    v_product(tile(1))

            pipeline(pe, STAGES, TILES, step, 2)

            pe.wait_ge(s["base_full"], TILES)
            pe.wait_ge(table_step, TABLE_STEPS)
            for i in range(2):
                last = mm(ps_tab[:, i * SLOTS:(i + 1) * SLOTS], of_tile[0:SLOTS, i:i + 1], ident[0:SLOTS, 0:SLOTS],
                          start=True, stop=True)
            last.then_inc(table_turned, 1)

            pe.wait_ge(table_ready, 1)
            pe.wait_ge(setup_dve, 4)
            pe.wait_ge(experts_in, 16 * 3 * EXPERTS)
            pe.wait_ge(s["base_full"], TILES)
            pe.wait_ge(s["row_i_ready"], TILES)

            def turn_rows(j, buf, count):
                pe.wait_ge(rows_in[buf], count)
                wait(pe, r["rT_ready"], j)
                for c in range(2):
                    last = turn(ps_rT[:, c, :], rows[buf][:, c * HALF:(c + 1) * HALF], ident)
                last.then_inc(r["rows_turned"], 1)

            def first_layer(j, buf, expert, part, dst, free, done):
                wait(pe, r[free], j - 1)
                a = part * INNER
                for c, k in ((0, HALF), (1, HALF + 1)):
                    last = mm(dst[buf % 2][:, 0:INNER], rT[buf % 2][0:k, c, :],
                              w1_sb[0:k, c, bass.ds(expert, 1), a:a + INNER].rearrange("p a f -> p (a f)"),
                              start=(c == 0), stop=(c == 1))
                last.then_inc(r[done], 1)

            def turn_act(j, buf):
                pe.wait_ge(r["act_ready"], j + 1)
                wait(pe, r["aT_ready"], j - 1)
                for c in range(ICH):
                    last = turn(ps_aT[buf % 2][:, c * P:(c + 1) * P], act_sb[buf % 2][:, c * P:(c + 1) * P], ident)
                last.then_inc(r["act_turned"], 1)

            def second_layer(j, buf, expert):
                pe.wait_ge(r["aT_ready"], j + 1)
                wait(pe, r["y_out_ready"], j)
                for c in range(ICH):
                    last = mm(ps_yo, aT[buf % 2][:, c, :],
                              w2_sb[:, bass.ds(expert, 1), c, :].rearrange("p a f -> p (a f)"),
                              start=(c == 0), stop=(c == ICH - 1))
                last.then_inc(r["experts_done"], 1)

            def expert_of(j):
                return pe.value_load(table_i[0:1, 0, bass.ds(j, 1)], min_val=0, max_val=EXPERTS - 1)

            held = {}

            def r_step(tile, seen, n):
                b0, b1_, b2_ = n % NX, (n - 1) % NX, (n - 2) % NX
                if n == 0:
                    held.clear()

                def hold(back):
                    if tile(back) is not None and n - back not in held:
                        held[n - back] = expert_of(tile(back))

                hold(1)
                if tile(1) is not None:
                    pe.wait_ge(r["rT_ready"], tile(1) + 1)
                    first_layer(tile(1), b1_, held[n - 1], 0, ps_glu, "glu_ready", "glu_done")
                hold(2)
                if tile(2) is not None:
                    turn_act(tile(2), b2_)
                if tile(0) is not None:
                    j = tile(0)
                    turn_rows(j, b0, 16 * (j // NX + 1) if isinstance(j, int) else (j - b0) * 4 + 16)
                if tile(1) is not None:
                    first_layer(tile(1), b1_, held[n - 1], 1, ps_lin, "lin_ready", "lin_done")
                if tile(0) is not None and (isinstance(tile(0), int) or n < NX - 1):
                    held[n] = expert_of(tile(0))
                if tile(2) is not None:
                    second_layer(tile(2), b2_, held[n - 2])

            pipeline(pe, R_STAGES, SLOTS, r_step, NX)

        @block.scalar
        def _(act):
            def copy(dst, src):
                return nc.scalar.activation(dst, src, ACT.Copy)

            for tile_T in (xnT, tT):
                act.wait_ge(setup_pool, 1)
                copy(tile_T[HALF:HALF + 1, 1, :], ones_bf[HALF:HALF + 1, :]).then_inc(setup_act, 1)

            def move(t, dst, src, done, free, ready):
                act.wait_ge(s[done], t + 1)
                wait(act, s[free], t)
                copy(dst, src).then_inc(s[ready], 1)

            def spread_keys(t):
                act.wait_ge(s["k_turned"], t + 1)
                wait(act, s["scores_done"], t)
                for h in range(HH):
                    last = nc.scalar.activation(
                        k_spread[:, :, :, h], ps_kT.rearrange("p c (j i k) -> p c j i k", j=PAIRS, i=2),
                        ACT.Copy, scale=const("head", HALF)[:, h:h + 1])
                last.then_inc(s["k_spread_ready"], 1)

            def spread_probs(t):
                act.wait_ge(s["pT_ready"], t + 1)
                wait(act, s["pv_done"], t)
                for j in range(PAIRS):
                    a = j * GROUP
                    last = copy(p_spread[a:a + GROUP, :, a:a + GROUP], pT[a:a + GROUP])
                last.then_inc(s["p_spread_ready"], 1)

            def step(tile, seen, n):
                if tile(6) is not None:
                    t, buf = tile(6), (n - 6) % 2
                    act.wait_ge(s["t_row_ready"], t + 1)
                    wait(act, scattered[buf], rows_out(t, buf))
                    copy(packet[buf][:, 0:DIM], t_row[buf][:]).then_inc(s["packed"], 1)
                if tile(1) is not None:
                    move(tile(1), xnT[0:HALF], ps_xT, "xn_turned", "v_done", "xnT_ready")
                if tile(2) is not None:
                    move(tile(2), qT[:], ps_qT, "q_turned", "scores_done", "qT_ready")
                if tile(2) is not None:
                    spread_keys(tile(2))
                if tile(5) is not None:
                    move(tile(5), tT[0:HALF], ps_tT, "t_turned", "gated", "tT_ready")
                if tile(3) is not None:
                    spread_probs(tile(3))
                if tile(6) is not None:
                    move(tile(6), combT[:], ps_cT, "comb_turned", "b2_done", "combT_ready")
                if tile(4) is not None:
                    t = tile(4)
                    act.wait_ge(s["x2_ready"], t + 1)
                    wait(act, s["msq_ready"], t)
                    nc.scalar.activation(x2sq[:], x2[:], ACT.Square, accum_out=ssq[:]).then_inc(s["ssq_ready"], 1)
                if tile(3) is not None:
                    move(tile(3), yT[:], ps_yT, "pv_done", "proj_done", "yT_ready")
                if tile(2) is not None:
                    t = tile(2)
                    act.wait_ge(s["sc2_ready"], t + 1)
                    wait(act, s["p_pair_ready"], 2 * t)
                    wait(act, s["rsum_ready"], t)
                    nc.scalar.activation(prob[:], sc2[:], ACT.Exp).then_inc(s["prob_ready"], 1)
                if tile(5) is not None:
                    t = tile(5)
                    act.wait_ge(s["top_d_ready"], t + 1)
                    wait(act, s["top_w_ready"], t)
                    nc.scalar.activation(top_e[:], top_d[:], ACT.Exp, accum_out=esum[:]).then_inc(s["top_e_ready"], 1)
                if tile(1) is not None:
                    t = tile(1)
                    act.wait_ge(s["v_done"], t + 1)
                    wait(act, s["pv_done"], t - 1)
                    copy(v_sb[:, (n - 1) % 2, 0:DIM], ps_v).then_inc(s["v_ready"], 1)

            pipeline(act, STAGES, TILES, step, 2)
            pad_regions(act, 1)
            nc.scalar.activation(x2sq[:, 0:1], power[:], ACT.Sigmoid)

            def r_step(tile, seen, n):
                if tile(2) is not None:
                    j, b = tile(2), n % 2
                    act.wait_ge(r["act_turned"], j + 1)
                    wait(act, r["experts_done"], j - 1)
                    copy(aT[b].rearrange("p c t -> p (c t)"), ps_aT[b][:, 0:INNER]).then_inc(r["aT_ready"], 1)
                if tile(0) is not None:
                    j, b = tile(0), n % 2
                    act.wait_ge(r["rows_turned"], j + 1)
                    wait(act, r["lin_done"], j - 1)
                    copy(rT[b][0:HALF], ps_rT).then_inc(r["rT_ready"], 1)
                if tile(1) is not None:
                    j, b = tile(1), (n - 1) % 2
                    act.wait_ge(r["glu_ready"], j + 1)
                    wait(act, r["act_ready"], j - 1)
                    nc.scalar.activation(sig[b], glu[b], ACT.Sigmoid, scale=ALPHA).then_inc(r["sig_ready"], 1)

            pipeline(act, R_STAGES, SLOTS, r_step, NX)

        @block.vector
        def _(dve):
            V = nc.vector
            V.memset(chosen_before[:], 0.0).then_inc(s["chosen_before_ready"], 1)
            dve.wait_ge(consts_in, 16)
            V.tensor_copy(before_bf[:], const("before")).then_inc(setup_dve, 1)
            V.tensor_copy(token_i[:], const("token")).then_inc(setup_dve, 1)
            dve.wait_ge(setup_pool, 2)
            V.tensor_copy(pad_row[:, ID_AT:ID_AT + 1].bitcast(I32), const("pad")).then_inc(pad_done, 1)
            dve.wait_ge(setup_pool, 3)
            dve.wait_ge(wsmall_in, 16 * 6)

            pke = [P, TOPK, EXPERTS]
            phk = [P, HEADS, SEQ]

            def h0_of(t):
                return h0[:, bass.ds(t, 1), :].rearrange("p a d -> p (a d)")

            def embed_add(t):
                dve.wait_ge(s["embedded"], t + 1)
                V.tensor_tensor(h0_of(t), ps_e, btok_bc[:], ALU.add).then_inc(s["h0_ready"], 1)

            def embed_stats(t):
                dve.wait_ge(s["h0_ready"], t + 1)
                alone(dve)
                V.bn_stats(stats1[:], h0_of(t)).then_inc(s["stats1_ready"], 1)

            def embed_aggr(t):
                dve.wait_ge(s["stats1_ready"], t + 1)
                alone(dve)
                V.bn_aggr(mv1[:], stats1[:]).then_inc(s["mv1_ready"], 1)

            def norm(t):
                dve.wait_ge(s["rstd1_ready"], t + 1)
                wait(dve, s["xn_turned"], t)
                V.tensor_scalar(xn[:], h0_of(t), mv1[:, 0:1], rstd1[:], ALU.subtract, ALU.mult
                                ).then_inc(s["xn_ready"], 1)

            def rope_products(t):
                dve.wait_ge(s["qk_done"], t + 1)
                view = ps_qk.rearrange("p (h f u) -> p h f u", h=2 * HEADS, u=2)
                cos = const("cos").unsqueeze(1).to_broadcast([P, 2 * HEADS, HD])
                sin = const("sin").rearrange("p (f u) -> p f u", u=2).unsqueeze(1).to_broadcast(
                    [P, 2 * HEADS, HD // 2, 2])
                V.tensor_tensor(rope_c[:].rearrange("p (h d) -> p h d", d=HD),
                                ps_qk.rearrange("p (h d) -> p h d", d=HD), cos, ALU.mult
                                ).then_inc(s["rope_c_ready"], 1)
                V.tensor_tensor(rope_s[:].rearrange("p (h f u) -> p h f u", h=2 * HEADS, u=2),
                                view[:, :, :, ::-1], sin, ALU.mult).then_inc(s["rope_s_ready"], 1)

            def rope_add(t):
                dve.wait_ge(s["rope_s_ready"], t + 1)
                wait(dve, s["k_turned"], t)
                V.tensor_tensor(qk[:], rope_c[:], rope_s[:], ALU.add).then_inc(s["qk_ready"], 1)

            def score_first(t):
                dve.wait_ge(s["scores_done"], t + 1)
                of_pair = ps_s.rearrange("p (h i k) -> p h i k", h=HEADS, i=2)
                V.scalar_tensor_tensor(half_s[:], of_pair[:, :, 0], const("own")[:, 0:1],
                                       const("causal").unsqueeze(1).to_broadcast(phk), ALU.mult, ALU.add
                                       ).then_inc(s["half_s_ready"], 1)

            def score_second(t):
                of_pair = ps_s.rearrange("p (h i k) -> p h i k", h=HEADS, i=2)
                dve.wait_ge(s["half_s_ready"], t + 1)
                V.scalar_tensor_tensor(sc1[:], of_pair[:, :, 1], const("own")[:, 1:2], half_s[:], ALU.mult, ALU.add
                                       ).then_inc(s["sc1_ready"], 1)

            def score_max(t):
                dve.wait_ge(s["sc1_ready"], t + 1)
                V.tensor_reduce(rmax[:], sc1[:], AX_X, ALU.max).then_inc(s["rmax_ready"], 1)

            def score_minus_max(t):
                dve.wait_ge(s["rmax_ready"], t + 1)
                wait(dve, s["prob_ready"], t)
                V.tensor_tensor(sc2[:], sc1[:], rmax[:].unsqueeze(2).to_broadcast(phk), ALU.subtract
                                ).then_inc(s["sc2_ready"], 1)

            def prob_sum(t):
                dve.wait_ge(s["prob_ready"], t + 1)
                V.tensor_reduce(rsum[:], prob[:], AX_X, ALU.add).then_inc(s["rsum_ready"], 1)

            def prob_inverse(t):
                dve.wait_ge(s["rsum_ready"], t + 1)
                V.reciprocal(rinv[:], rsum[:]).then_inc(s["rinv_done"], 1)

            def prob_inverse_own(t):
                dve.wait_ge(s["rinv_done"], t + 1)
                wait(dve, s["p_pair_ready"], 2 * t)
                V.tensor_tensor(rinv_own[:], rinv[:].unsqueeze(1).to_broadcast([P, 2, HEADS]),
                                const("odd").unsqueeze(2).to_broadcast([P, 2, HEADS]), ALU.mult
                                ).then_inc(s["rinv_ready"], 1)

            def turn_probs(t):
                dve.wait_ge(s["p_pair_ready"], 2 * (t + 1))
                wait(dve, s["p_spread_ready"], t)
                V.transpose(pT[:].rearrange("p h q -> p (h q)"), p_pair[:].rearrange("p h i k -> p (h i k)")
                            ).then_inc(s["pT_ready"], 1)

            def attn_add(t):
                dve.wait_ge(s["proj_done"], t + 1)
                wait(dve, s["base_ready"], t)
                V.tensor_tensor(h1[:], ps_p, h0_of(t), ALU.add).then_inc(s["h1_ready"], 1)

            def attn_stats(t):
                dve.wait_ge(s["h1_ready"], t + 1)
                alone(dve)
                V.bn_stats(stats2[:], h1[:]).then_inc(s["stats2_ready"], 1)

            def attn_aggr(t):
                dve.wait_ge(s["stats2_ready"], t + 1)
                alone(dve)
                V.bn_aggr(mv2[:], stats2[:]).then_inc(s["mv2_ready"], 1)

            def norm2(t):
                dve.wait_ge(s["rstd2_ready"], t + 1)
                wait(dve, s["ssq_ready"], t)
                V.tensor_scalar(x2[:], h1[:], mv2[:, 0:1], rstd2[:], ALU.subtract, ALU.mult
                                ).then_inc(s["x2_ready"], 1)

            def norm3(t, buf):
                dve.wait_ge(s["rms_ready"], t + 1)
                dve.wait_ge(s["x2_ready"], t + 1)
                wait(dve, s["t_turned"], t - 1)
                wait(dve, s["packed"], t - 1)
                V.scalar_tensor_tensor(t_row[buf][:], x2[:], rms[:], nscale_bc[:], ALU.mult, ALU.mult
                                       ).then_inc(s["t_row_ready"], 1)

            def top_max(t):
                dve.wait_ge(s["gated"], t + 1)
                alone(dve)
                V.max(top_v[:], ps_g).then_inc(s["top_v_ready"], 1)

            def top_index(t):
                dve.wait_ge(s["top_v_ready"], t + 1)
                alone(dve)
                V.max_index(top_i[:], top_v[:], ps_g).then_inc(s["top_i_ready"], 1)
                wait(dve, s["top_e_ready"], t)
                V.tensor_scalar(top_d[:], top_v[:, 0:TOPK], top_v[:, 0:1], None, ALU.subtract
                                ).then_inc(s["top_d_ready"], 1)

            def top_float(t):
                dve.wait_ge(s["top_i_ready"], t + 1)
                V.tensor_copy(top_f[:], top_i[:, 0:TOPK]).then_inc(s["top_f_ready"], 1)

            def mark_experts(t):
                dve.wait_ge(s["top_f_ready"], t + 1)
                V.tensor_tensor(onehot[:], const("expert").unsqueeze(1).to_broadcast(pke),
                                top_f[:].unsqueeze(2).to_broadcast(pke), ALU.is_equal
                                ).then_inc(s["onehot_ready"], 1)

            def choose_experts(t):
                dve.wait_ge(s["top_e_ready"], t + 1)
                V.reciprocal(einv[:], esum[:]).then_inc(s["einv_ready"], 1)
                dve.wait_ge(s["onehot_ready"], t + 1)
                wait(dve, s["ranked"], t)
                with nc.allow_low_precision("counts of zero or one are exact"):
                    V.tensor_reduce(chosen[:], onehot[:].rearrange("p k e -> p e k"), AX_X, ALU.add
                                    ).then_inc(s["chosen_ready"], 1)

            def top_weights(t):
                dve.wait_ge(s["einv_ready"], t + 1)
                V.tensor_scalar(top_w[:], top_e[:], einv[:], None, ALU.mult).then_inc(s["top_w_ready"], 1)

            def weigh_experts(t):
                dve.wait_ge(s["top_w_ready"], t + 1)
                V.tensor_tensor(onehot_w[:], onehot[:], top_w[:].unsqueeze(2).to_broadcast(pke), ALU.mult
                                ).then_inc(s["onehot_w_ready"], 1)

            def combine(t):
                dve.wait_ge(s["onehot_w_ready"], t + 1)
                wait(dve, s["comb_turned"], t)
                V.tensor_reduce(comb[:], onehot_w[:].rearrange("p k e -> p e k"), AX_X, ALU.add
                                ).then_inc(s["comb_ready"], 1)

            def fill_packet(t, buf):
                dve.wait_ge(s["comb_ready"], t + 1)
                wait(dve, scattered[buf], rows_out(t, buf))
                V.tensor_copy(packet[buf][:, W_AT:W_AT + EXPERTS], comb[:]).then_inc(s["weights_ready"], 1)
                V.tensor_copy(packet[buf][:, ID_AT:ID_AT + 1].bitcast(I32), token_i[:, bass.ds(t, 1)]
                              ).then_inc(s["token_ready"], 1)

            def place_all(t):
                dve.wait_ge(s["ranked"], t + 1)
                V.tensor_tensor(place[:], ps_r, const("region"), ALU.add).then_inc(s["place_ready"], 1)
                V.tensor_tensor(chosen_before[:], chosen_before[:], chosen[:], ALU.add
                                ).then_inc(s["chosen_before_ready"], 1)

            def place_chosen(t):
                dve.wait_ge(s["place_ready"], t + 1)
                V.tensor_tensor(onehot_r[:], onehot[:], place[:].unsqueeze(1).to_broadcast(pke), ALU.mult
                                ).then_inc(s["onehot_r_ready"], 1)

            def place_sum(t):
                dve.wait_ge(s["onehot_r_ready"], t + 1)
                V.tensor_reduce(row_f[:], onehot_r[:], AX_X, ALU.add).then_inc(s["row_f_ready"], 1)

            def place_whole(t, buf):
                dve.wait_ge(s["row_f_ready"], t + 1)
                wait(dve, scattered[buf], rows_out(t, buf))
                V.tensor_copy(row_i[buf][:], row_f[:]).then_inc(s["row_i_ready"], 1)

            def add_bias(t):
                dve.wait_ge(s["b2_done"], t + 1)
                dve.wait_ge(s["base_ready"], t + 1)
                bt = base[:, bass.ds(t, 1), :].rearrange("p a d -> p (a d)")
                V.tensor_tensor(bt, bt, ps_b, ALU.add).then_inc(s["base_full"], 1)

            def step(tile, seen, n):
                def at(stage, work, *buf):
                    if tile(stage) is not None:
                        work(tile(stage), *buf)

                par5, par6 = (n - 5) % 2, (n - 6) % 2
                at(3, prob_sum)
                at(6, mark_experts)
                at(6, choose_experts)
                at(6, top_weights)
                at(3, prob_inverse)
                at(3, prob_inverse_own)
                at(6, weigh_experts)
                if isinstance(tile(6), int) and tile(6) == TILES - 1:
                    dve.wait_ge(counted, 1)
                    V.tensor_tensor(fill_i[:], ps_cnt[0:1, :], const("region", 1), ALU.add).then_inc(fill_ready, 1)
                at(5, norm3, par5)
                at(6, combine)
                at(0, embed_add)
                at(0, embed_stats)
                at(6, fill_packet, par6)
                at(4, attn_add)
                at(0, embed_aggr)
                at(3, turn_probs)
                at(4, attn_stats)
                at(6, place_all)
                at(4, attn_aggr)
                at(0, norm)
                at(6, place_chosen)
                at(6, place_sum)
                at(6, place_whole, par6)
                at(5, top_max)
                at(1, rope_products)
                at(4, norm2)
                at(2, score_first)
                at(2, score_second)
                at(5, top_index)
                at(5, top_float)
                at(2, score_max)
                at(2, score_minus_max)
                at(1, rope_add)
                at(6, add_bias)

            pipeline(dve, STAGES, TILES, step, 2)
            for i in range(2):
                V.tensor_copy(rT[i][HALF:HALF + 1, 1, :], ones_bf[HALF:HALF + 1, :]).then_inc(setup_dve, 1)

            made = [0]

            def then_wait(instruction):
                instruction.then_inc(table_step, 1)
                made[0] += 1
                dve.wait_ge(table_step, made[0])

            then_wait(V.tensor_scalar(cnt_i[:], ps_cnt, float(P - 1), None, ALU.add))
            then_wait(V.tensor_scalar(cnt_i2[:], cnt_i[:], P.bit_length() - 1, None, ALU.logical_shift_right))
            then_wait(V.tensor_copy(ntile[:], cnt_i2[:]))
            then_wait(V.tensor_tensor_scan(tend[:], ones_f[:], ntile[:], 0.0, ALU.mult, ALU.add))
            then_wait(V.tensor_scalar(jump[:], ntile[:], -float(P), float(REGION), ALU.mult, ALU.add))
            then_wait(V.tensor_scalar(passed[:], tend[:], const("tile"), None, ALU.is_le))
            then_wait(V.tensor_tensor(jumped[:], passed[:], jump[:], ALU.mult))
            then_wait(V.tensor_reduce(of_tile[:, 2:3], passed[:], AX_X, ALU.add))
            then_wait(V.tensor_reduce(of_tile[:, 3:4], jumped[:], AX_X, ALU.add))
            then_wait(V.tensor_scalar(of_tile[:, 0:1], of_tile[:, 2:3], float(EXPERTS - 1), None, ALU.min))
            then_wait(V.scalar_tensor_tensor(of_tile[:, 2:3], const("tile"), float(P), of_tile[:, 3:4],
                                             ALU.mult, ALU.add))
            then_wait(V.tensor_scalar(of_tile[:, 1:2], of_tile[:, 2:3], float(SPARE), None, ALU.min))
            assert made[0] == TABLE_STEPS
            dve.wait_ge(table_turned, 1)
            V.tensor_copy(table_i[:].rearrange("p a j -> p (a j)"), ps_tab).then_inc(table_ready, 1)
            dve.wait_ge(table_ready, 1)

            def r_step(tile, seen, n):
                if tile(1) is not None:
                    j, b = tile(1), (n - 1) % 2
                    dve.wait_ge(r["glu_done"], j + 1)
                    wait(dve, r["sig_ready"], j - 1)
                    V.tensor_scalar(glu[b], ps_glu[b][:, 0:INNER], LIMIT, None, ALU.min
                                    ).then_inc(r["glu_ready"], 1)
                    dve.wait_ge(r["lin_done"], j + 1)
                    V.tensor_scalar(lin[b], ps_lin[b][:, 0:INNER], LIMIT, -LIMIT, ALU.min, ALU.max
                                    ).then_inc(r["lin_ready"], 1)
                    dve.wait_ge(r["lin_ready"], j + 1)
                    V.scalar_tensor_tensor(lin[b], lin[b], 1.0, glu[b], ALU.add, ALU.mult
                                           ).then_inc(r["gl_ready"], 1)
                    dve.wait_ge(r["gl_ready"], j + 1)
                    dve.wait_ge(r["sig_ready"], j + 1)
                    wait(dve, r["act_turned"], j - 1)
                    V.tensor_tensor(act_sb[b], lin[b], sig[b], ALU.mult).then_inc(r["act_ready"], 1)
                if tile(2) is not None:
                    j, b = tile(2), (n - 2) % NX
                    dve.wait_ge(r["experts_done"], j + 1)
                    wait(dve, r["added"], 16 * (j - NX + 2))
                    dve.wait_ge(r["noted"], 2 * (j + 1))
                    V.tensor_scalar(y_out[b], ps_yo, row_w[:, b:b + 1], None, ALU.mult
                                    ).then_inc(r["y_out_ready"], 1)

            pipeline(dve, R_STAGES, SLOTS, r_step, NX)

        @block.gpsimd
        def _(pool):
            G = nc.gpsimd
            G.memset(ones_bf[:], 1.0).then_inc(setup_pool, 1)
            G.memset(pad_row[:], 0.0).then_inc(setup_pool, 1)
            for buf in packet:
                G.memset(buf[:], 0.0)
            G.memset(p_spread[:], 0.0)
            G.memset(v_sb[:, :, DIM + 1:V_N], 0.0)
            G.memset(v_sb[:, :, DIM:DIM + 1], 1.0)
            G.memset(power[:], -0.5)
            G.memset(ones_f[:], 1.0).then_inc(setup_pool, 1)
            pool.wait_ge(setup_pool, 3)

            def inverse_root(t, var, scale, ready, tmp, tmp_ready, dst, free, dst_ready):
                pool.wait_ge(s[ready], t + 1)
                alone(pool)
                G.tensor_scalar(tmp[:], var, scale, EPS, ALU.mult, ALU.add).then_inc(s[tmp_ready], 1)
                pool.wait_ge(s[tmp_ready], t + 1)
                wait(pool, s[free], t)
                G.tensor_tensor(dst[:], tmp[:], power[:], ALU.pow).then_inc(s[dst_ready], 1)

            def scatter(t, buf):
                pool.wait_ge(s["row_i_ready"], t + 1)
                pool.wait_ge(s["packed"], t + 1)
                pool.wait_ge(s["weights_ready"], t + 1)
                pool.wait_ge(s["token_ready"], t + 1)
                alone(pool)
                for k in range(TOPK):
                    G.indirect_dma_start(out=routed, out_offset=bass.IndirectOffsetOnAxis(
                        ap=row_i[buf][:, k:k + 1].bitcast(U32), axis=0),
                                         in_=packet[buf][:], in_offset=None).then_inc(scattered[buf], 16)

            def residual(t):
                pool.wait_ge(s["x2_ready"], t + 1)
                G.tensor_tensor(base[:, bass.ds(t, 1), :].rearrange("p a d -> p (a d)"), h1[:], x2[:], ALU.add
                                ).then_inc(s["base_ready"], 1)

            def normalise(t):
                pool.wait_ge(s["rinv_ready"], t + 1)
                wait(pool, s["pT_ready"], t)
                for i in range(2):
                    G.tensor_tensor(p_pair[:, :, i], prob[:], rinv_own[:, i].unsqueeze(2).to_broadcast(
                        [P, HEADS, SEQ]), ALU.mult).then_inc(s["p_pair_ready"], 1)

            def step(tile, seen, n):
                if tile(3) is not None:
                    normalise(tile(3))
                if tile(0) is not None:
                    inverse_root(tile(0), mv1[:, 1:2], 1.0, "mv1_ready", ve1, "ve1_ready", rstd1, "xn_ready",
                                 "rstd1_ready")
                if tile(4) is not None:
                    inverse_root(tile(4), mv2[:, 1:2], 1.0, "mv2_ready", ve2, "ve2_ready", rstd2, "x2_ready",
                                 "rstd2_ready")
                if tile(6) is not None and tile(2) is not None:
                    scatter(tile(6), (n - 6) % 2)
                if tile(4) is not None:
                    inverse_root(tile(4), ssq[:], 1.0 / DIM, "ssq_ready", msq, "msq_ready", rms, "t_row_ready",
                                 "rms_ready")
                    residual(tile(4))
                if tile(6) is not None and tile(2) is None:
                    scatter(tile(6), (n - 6) % 2)

            pipeline(pool, STAGES, TILES, step, 2)
            pad_regions(pool, 2)
            pool.wait_ge(base_out, 16 * TILES)
            pool.wait_ge(dump_out, 16)
            pool.wait_ge(table_ready, 1)

            def r_step(tile, seen, n):
                if tile(1) is not None:
                    j, b = tile(1), (n - 1) % NX
                    e = pool.value_load(table_i[0:1, 0, bass.ds(j, 1)], min_val=0, max_val=EXPERTS - 1)
                    pool.wait_ge(rows_in[b], 16 * (j // NX + 1) if isinstance(j, int) else (j - b) * 4 + 16)
                    wait(pool, r["added"], 16 * (j - NX + 1))
                    alone(pool)
                    G.tensor_copy(row_w[:, b:b + 1], rows[b][:, bass.ds(e + W_AT, 1)]).then_inc(r["noted"], 1)
                    G.tensor_copy(row_id[:, b:b + 1], rows[b][:, ID_AT:ID_AT + 1].bitcast(I32)
                                  ).then_inc(r["noted"], 1)
                if tile(2) is not None:
                    j, b = tile(2), (n - 2) % NX
                    pool.wait_ge(r["y_out_ready"], j + 1)
                    wait(pool, r["added"], 16 * j)
                    alone(pool)
                    G.indirect_dma_start(out=out, out_offset=bass.IndirectOffsetOnAxis(
                        ap=row_id[:, b:b + 1].bitcast(U32), axis=0),
                        in_=y_out[b], in_offset=None, compute_op=ALU.add).then_inc(r["added"], 16)

            pipeline(pool, R_STAGES, SLOTS, r_step, NX)


def kernel(x, L0_tok_W, L0_tok_b, L0_attn_W_attn, L0_attn_b_attn, L0_attn_W_proj, L0_attn_b_proj,
           L0_ffn_norm_scale, L0_ffn_gate_w, L0_ffn_gate_b, L0_ffn_mlp1_w, L0_ffn_mlp1_b, L0_ffn_mlp2_w,
           L0_ffn_mlp2_b):
    import concourse.bacc as bacc
    from concourse.bass_utils import run_bass_kernel_spmd

    def lay(a, *shape):
        return np.ascontiguousarray(a).reshape(shape)

    def halves(w):
        return np.ascontiguousarray(np.asarray(w).reshape(2, HALF, -1).transpose(1, 0, 2))

    x = np.asarray(x)
    side, w = 4, 16
    patches = x.reshape(TILES, IMGS, 3, side, w, side, w).transpose(0, 4, 6, 2, 1, 3, 5)
    patches = patches.reshape(TILES, PCH, P, P).transpose(0, 2, 1, 3)
    w_tok = np.asarray(L0_tok_W).T.reshape(PCH, P, DIM).transpose(1, 0, 2)
    w1 = np.asarray(L0_ffn_mlp1_w).reshape(EXPERTS, INNER, 2, 2, HALF).transpose(4, 3, 0, 2, 1)
    b1 = np.asarray(L0_ffn_mlp1_b).reshape(1, EXPERTS, INNER, 2).transpose(0, 1, 3, 2)
    w2 = np.asarray(L0_ffn_mlp2_w).reshape(EXPERTS, DIM, ICH, P).transpose(3, 0, 2, 1)
    w_proj = np.zeros((P // GROUP, GROUP, YCH, DIM), np.float32)
    w_proj[:, 0:HD] = np.asarray(L0_attn_W_proj).reshape(YCH, P // GROUP, HD, DIM).transpose(1, 2, 0, 3)
    w_proj[-1, HD, -1] = np.asarray(L0_attn_b_proj)
    w_proj = w_proj.reshape(P, YCH, DIM)
    arrays = {
        "patches": lay(patches, TILES, P, PCH, P),
        "consts": shape_constants(),
        "w_tok": lay(w_tok, P, PCH, DIM),
        "b_tok": lay(L0_tok_b, 1, DIM),
        "w_qkv": halves(L0_attn_W_attn),
        "b_qkv": lay(L0_attn_b_attn, 1, 3 * DIM),
        "w_proj": w_proj,
        "nscale": lay(L0_ffn_norm_scale, 1, DIM),
        "w_gate": halves(np.asarray(L0_ffn_gate_w).T),
        "b_gate": lay(L0_ffn_gate_b, 1, EXPERTS),
        "w1": lay(w1, HALF, 2, EXPERTS, 2 * INNER),
        "b1": lay(b1, 1, EXPERTS, 2 * INNER),
        "w2": lay(w2, P, EXPERTS, ICH, DIM),
        "b2": lay(L0_ffn_mlp2_b, EXPERTS, DIM),
    }
    nc = bacc.Bacc("TRN2", target_bir_lowering=False, num_devices=1)
    args = [nc.dram_tensor(n, a.shape, F32, kind="ExternalInput").ap() for n, a in arrays.items()]
    out = nc.dram_tensor("out_rows", (TOKENS + P, DIM), F32, kind="ExternalOutput").ap()
    build(nc, *args, out)
    result = run_bass_kernel_spmd(nc, [arrays], core_ids=[0])
    return result.results[0]["out_rows"][:TOKENS].reshape(TILES * IMGS, SEQ, DIM)
```
